# Optimizing a Trainium2 kernel written in Bass

```python
import numpy as np
import jax
import jax.numpy as jnp

def _softmax(x, axis=-1):
    return jax.nn.softmax(x, axis=axis)

def _gelu(x):
    return jax.nn.gelu(x, approximate=True)

def _silu(x):
    return jax.nn.silu(x)

def _sigmoid(x):
    return jax.nn.sigmoid(x)

def _layernorm(x, axis=-1, eps=1e-05):
    m = jnp.mean(x, axis=axis, keepdims=True)
    v = jnp.var(x, axis=axis, keepdims=True)
    return (x - m) / jnp.sqrt(v + eps)

def _scatter_add(tgt, idx, src, axis=0):
    return tgt.at[idx].add(src)

def _segment_sum(src, seg, n):
    return jax.ops.segment_sum(src, seg, n)
kernel_name = 'mk_xattn_seq_d2_seqx_r4_763e9c'

def setup_inputs(seed: int=0):
    np.random.seed(seed)
    _w = jnp.asarray

    def _rec_inputs():
        import jax
        import jax.numpy as jnp
        _rk = jax.random.key(seed)
        x = -0.0003929 + 0.9999 * jax.random.normal(jax.random.fold_in(_rk, 1), (4, 1024, 256), jnp.float32)
        _lenS = 1024 - jax.random.randint(jax.random.fold_in(_rk, 7), (4,), 0, max(1, 1024 // 4) + 1, jnp.int32)
        _lenS2 = 154 - jax.random.randint(jax.random.fold_in(_rk, 8), (4,), 0, max(1, 154 // 4) + 1, jnp.int32)
        _ctx_1024P = jax.random.normal(jax.random.fold_in(_rk, 11), (4, 16, 256), jnp.float32)
        _ctx_1024c = jax.random.dirichlet(jax.random.fold_in(_rk, 511), 0.3 * jnp.ones((16,), jnp.float32), (4, 154))
        _ctx_1024t = jnp.einsum('bsk,bkd->bsd', _ctx_1024c, _ctx_1024P)
        _ctx_1024t = _ctx_1024t * jax.lax.rsqrt(jnp.mean(jnp.square(_ctx_1024t)) + 1e-12) * 0.953939
        ctx_1024 = 2.81802e-05 + 1.00001 * (_ctx_1024t + 0.3 * jax.random.normal(jax.random.fold_in(_rk, 611), (4, 154, 256), jnp.float32))
        return (x, ctx_1024)
    x, ctx_1024 = _rec_inputs()

    def _L0_xattn_setup():
        import jax, jax.numpy as jnp
        import numpy as np
        EMBED = 256
        key = jax.random.key(seed)
        k1, k2, k3, k4, k5 = jax.random.split(key, 5)
        B, Sl, Sr, D = (4, 1024, 1024, EMBED)
        left = jax.random.normal(k1, (B, Sl, D), dtype=jnp.float32)
        right = jax.random.normal(k2, (B, Sr, D), dtype=jnp.float32)
        scale = 1.0 / np.sqrt(D)
        Wq = jax.random.normal(k3, (D, D), dtype=jnp.float32) * scale
        Wk = jax.random.normal(k4, (D, D), dtype=jnp.float32) * scale
        Wv = jax.random.normal(k5, (D, D), dtype=jnp.float32) * scale
        return {'left': left, 'right': right, 'Wq': Wq, 'Wk': Wk, 'Wv': Wv}
    _L0_xattn_all = _L0_xattn_setup()
    _L0_xattn_in = {k: v for k, v in _L0_xattn_all.items() if k in ('Wq', 'Wk', 'Wv')}
    del _L0_xattn_all

    def _L1_xattn_setup():
        import jax, jax.numpy as jnp
        import numpy as np
        D_MODEL = 256
        H = 16
        D_K = 64
        D_V = 64
        NEG_INF = -1000000000.0
        LN_EPS = 1e-05
        key = jax.random.key(seed)
        ks = jax.random.split(key, 7)
        B, S = (4, 512)
        scale = 1.0 / np.sqrt(D_MODEL)
        return {'Q': jax.random.normal(ks[0], (B, S, D_MODEL), jnp.float32), 'K': jax.random.normal(ks[1], (B, S, D_MODEL), jnp.float32), 'V': jax.random.normal(ks[2], (B, S, D_MODEL), jnp.float32), 'W_Q': jax.random.normal(ks[3], (D_MODEL, D_K * H), jnp.float32) * scale, 'W_K': jax.random.normal(ks[4], (D_MODEL, D_K * H), jnp.float32) * scale, 'W_V': jax.random.normal(ks[5], (D_MODEL, D_V * H), jnp.float32) * scale, 'W_O': jax.random.normal(ks[6], (D_V * H, D_MODEL), jnp.float32) * scale, 'ln_gamma': jnp.ones((D_MODEL,), jnp.float32), 'ln_beta': jnp.zeros((D_MODEL,), jnp.float32)}
    _L1_xattn_all = _L1_xattn_setup()
    _L1_xattn_in = {k: v for k, v in _L1_xattn_all.items() if k in ('W_Q', 'W_K', 'W_V', 'W_O', 'ln_gamma', 'ln_beta')}
    del _L1_xattn_all
    return {'x': x, 'ctx_1024': ctx_1024, 'L0_xattn_Wq': _L0_xattn_in['Wq'], 'L0_xattn_Wk': _L0_xattn_in['Wk'], 'L0_xattn_Wv': _L0_xattn_in['Wv'], 'L1_xattn_W_Q': _L1_xattn_in['W_Q'], 'L1_xattn_W_K': _L1_xattn_in['W_K'], 'L1_xattn_W_V': _L1_xattn_in['W_V'], 'L1_xattn_W_O': _L1_xattn_in['W_O'], 'L1_xattn_ln_gamma': _L1_xattn_in['ln_gamma'], 'L1_xattn_ln_beta': _L1_xattn_in['ln_beta']}

def reference(x, ctx_1024, L0_xattn_Wq, L0_xattn_Wk, L0_xattn_Wv, L1_xattn_W_Q, L1_xattn_W_K, L1_xattn_W_V, L1_xattn_W_O, L1_xattn_ln_gamma, L1_xattn_ln_beta):
    import jax
    import jax.numpy as jnp

    def _L0_xattn_ref(left, right, Wq, Wk, Wv):
        import jax, jax.numpy as jnp
        import numpy as np
        EMBED = 256
        q = jnp.einsum('bip,pd->bid', left, Wq)
        k = jnp.einsum('bjp,pd->bjd', right, Wk)
        v = jnp.einsum('bjp,pd->bjd', right, Wv)
        d = q.shape[-1]
        scores = jnp.einsum('bip,bjp->bij', q, k) * d ** (-0.5)
        attn = jax.nn.softmax(scores, axis=-1)
        out = jnp.einsum('bis,bsj->bij', attn, v)
        return out + left

    def _L1_xattn_ref(Q, K, V, W_Q, W_K, W_V, W_O, ln_gamma, ln_beta):
        import jax, jax.numpy as jnp
        import numpy as np
        D_MODEL = 256
        H = 16
        D_K = 64
        D_V = 64
        NEG_INF = -1000000000.0
        LN_EPS = 1e-05
        B, Lq, _ = Q.shape
        Lk = K.shape[1]
        Qh = (Q @ W_Q).reshape(B, Lq, H, D_K).transpose(0, 2, 1, 3)
        Kh = (K @ W_K).reshape(B, Lk, H, D_K).transpose(0, 2, 1, 3)
        Vh = (V @ W_V).reshape(B, Lk, H, D_V).transpose(0, 2, 1, 3)
        scores = jnp.einsum('bhqd,bhkd->bhqk', Qh, Kh) / jnp.sqrt(jnp.float32(D_K))
        mask = jnp.triu(jnp.full((Lq, Lk), NEG_INF, jnp.float32), k=1)
        scores = scores + mask
        attn = jax.nn.softmax(scores, axis=-1)
        ctx = jnp.einsum('bhqk,bhkd->bhqd', attn, Vh)
        ctx = ctx.transpose(0, 2, 1, 3).reshape(B, Lq, H * D_V)
        out = ctx @ W_O
        x = Q + out
        mu = jnp.mean(x, axis=-1, keepdims=True)
        var = jnp.mean(jnp.square(x - mu), axis=-1, keepdims=True)
        return (x - mu) * jax.lax.rsqrt(var + LN_EPS) * ln_gamma + ln_beta
    x = _L0_xattn_ref(x, ctx_1024, L0_xattn_Wq, L0_xattn_Wk, L0_xattn_Wv)
    x = _L1_xattn_ref(x, ctx_1024, ctx_1024, L1_xattn_W_Q, L1_xattn_W_K, L1_xattn_W_V, L1_xattn_W_O, L1_xattn_ln_gamma, L1_xattn_ln_beta)
    return x

_drawn_inputs = setup_inputs


def setup_inputs(seed=0):
    import zlib

    import numpy as np

    out = dict(_drawn_inputs(seed))
    spreads = {'L1_xattn_ln_gamma': (1.0, 0.2), 'L1_xattn_ln_beta': (0.0, 0.1)}
    factors = {}
    for name, (base, spread) in spreads.items():
        noise = np.random.default_rng([zlib.crc32(name.encode()), seed]).standard_normal(out[name].shape)
        drawn = base * np.exp(spread * noise) if base else spread * noise
        out[name] = jnp.asarray(drawn.astype(out[name].dtype))
    for name, factor in factors.items():
        out[name] = (out[name] * factor).astype(out[name].dtype)
    return out
```

```python
import concourse.bass as bass
from concourse import mybir
from contextlib import ExitStack

F32 = mybir.dt.float32
F32R = mybir.dt.float32r
ALU = mybir.AluOpType
ACT = mybir.ActivationFunctionType
AX = mybir.AxisListType

P = 128
B, S, J, D = 4, 1024, 154, 256
H, DK = 16, 64
KD = D // P
JT = J - P
TR = 32
JP = P + TR
JW = 192
CH = 512
NT = CH // P
NC = B * S // CH
G = 4
HG = H // G
NS = G * NT
PAIR = 2 * DK
EPS = 1e-5
MASKED = -1.0e9
ZEROED, BLANKED = 6, 5
BANKS = 3


PLACES = ("first", "mid", "last")
KV_STEPS = ((2, 5, 9, 13), (2, 6, 10, 14))
CTX_STEP, X_STEP = 0, 1
PROJECT_STEPS = (7, 8)
NORM_STEPS = (4, 5)


def step_jobs(c, s):
    own, prev, nxt = 0 <= c < NC, 1 <= c <= NC, -1 <= c < NC - 1
    second = c % 2 == 1
    b = c // 2
    at = {place: [] for place in PLACES}
    if nxt and second and s == 0:
        at["mid"].append(("values0", b + 1))
        at["last"].append(("mix0", b + 1))
    if nxt:
        for kind, start in (("turn_y", 4), ("attend0", 3), ("turn_p0", 2), ("scores0", 1)):
            t, between = divmod(s - start, 2)
            if 0 <= t < NT and not between:
                at["mid"].append((kind, c + 1, t))
    if s % 2 == 0:
        g, pair = divmod(s // 2 - 2, 2)
        if g >= 0 and own:
            at["first"].append(("attend", c, g, pair))
        if g < 0 and prev:
            at["first"].append(("attend", c - 1, G + g, pair))
    else:
        g, pair = divmod((s + 5) // 2, 2)
        if g < G and own:
            at["first"].append(("queries", c, g, pair))
        if g >= G and nxt:
            at["first"].append(("queries", c + 1, g - G, pair))
    for half in range(2):
        g, r = divmod(s - PROJECT_STEPS[half], NT)
        if r == 0 and g >= 0 and own:
            at["last"].append(("project", c, g, half))
        if r == 0 and g < 0 and prev:
            at["last"].append(("project", c - 1, g + G, half))
    if s in KV_STEPS[second]:
        g = KV_STEPS[second].index(s)
        if second and nxt:
            at["last"].append(("keys", b + 1, g))
        if not second and own:
            at["last"].append(("values", b, g))
    return at


SETUP_JOBS = [("fold0",)]
BY_DVE_ALONE = ("attend0", "project")


def number_jobs():
    order = list(SETUP_JOBS)
    for c in range(-1, NC + 1):
        for s in range(NS):
            at = step_jobs(c, s)
            order += [job for place in PLACES for job in at[place]]
    return ({job: k for k, job in enumerate(order)},
            {job: k for k, job in enumerate(j for j in order if j[0] not in BY_DVE_ALONE)})


JOB, ACT_JOB = number_jobs()


def bank_of(job):
    return JOB[job] % BANKS


class Period:

    def __init__(self, c0, i=None):
        self.c, self.i = c0, i

    def at(self, count):
        base = count(self.c)
        if self.i is None:
            return base
        rise = count(self.c + 2) - base
        assert count(self.c + 4) == base + 2 * rise
        return base + self.i * rise if rise else base

    def moved(self, job, c):
        by = c - self.c
        if not by:
            return job
        if job[0] in ("keys", "values", "values0", "mix0"):
            by //= 2
        return (job[0], job[1] + by) + job[2:]

    def done(self, job):
        return self.at(lambda c: JOB[self.moved(job, c)] + 1)

    def done_act(self, job):
        return self.at(lambda c: ACT_JOB[self.moved(job, c)] + 1)

    @property
    def own(self):
        return 0 <= self.c < NC

    @property
    def next(self):
        return -1 <= self.c < NC - 1

    def scored(self, s):
        if s + 2 < NS:
            return (self.c, s + 2) if self.own else None
        return (self.c + 1, s + 2 - NS) if self.next else None

    def summed(self, s):
        if s + 1 < NS:
            return (self.c, s + 1) if self.own else None
        return (self.c + 1, s + 1 - NS) if self.next else None

    def splits_weights(self, s):
        second = self.c % 2 == 1
        if s + 1 in KV_STEPS[second] and (self.next if second else self.own):
            return KV_STEPS[second].index(s + 1)
        return None

    def splits_ctx(self, s):
        return s == CTX_STEP and self.c % 2 == 1 and self.next

    def splits_x(self, s):
        return s == X_STEP and self.next


def kv_job_before(c, w):
    b = c // 2
    if c % 2 == 1:
        return ("keys", b + 1, w - 1) if w else ("values", b, G - 1)
    return ("values", b, w - 1) if w else ("keys", b, G - 1)


def run_periods(engine, period):
    period(Period(-1))
    period(Period(0))
    with engine.Fori(0, (NC - 2) // 2) as i:
        period(Period(1, i))
        period(Period(2, i))
    period(Period(NC - 1))
    period(Period(NC))


def cross_attention(nc, xT, x, ctxT, wq0T, wk0T, wv0, wq, wk, wv, wo, gamma, beta, out):
    es = ExitStack()
    with es:
        def sb(name, shape, dt=F32):
            return es.enter_context(nc.sbuf_tensor(name, shape, dt))

        def sem(name):
            return es.enter_context(nc.semaphore(name))

        def split(name, shape):
            return sb(name + "_hi", shape, F32R), sb(name + "_lo", shape, F32R)

        xT_raw = sb("xT_raw", [P, KD, CH])
        x_rows = sb("x_rows", [P, NT, D])
        ctx_raw = sb("ctx_raw", [P, KD, JW])
        wkv_raw = sb("wkv_raw", [P, 2, KD, D])
        gamma_b = sb("gamma_b", [P, D])
        beta_b = sb("beta_b", [P, D])
        xs = split("xs", [P, KD, CH])
        ctx = split("ctx", [P, KD, JW])
        ctx_tail = split("ctx_tail", [P, KD, HG, TR])
        wkv = split("wkv", [P, KD, D])
        wq_s = split("wq", [P, KD, H * DK])
        wo_s = split("wo", [P, H * DK // P, D])
        wv0_s = split("wv0", [P, KD, D])
        fold = split("fold", [P, KD, D])
        mix = split("mix", [P, KD, JW])
        v0 = split("v0", [P, D])
        v0_tail = sb("v0_tail", [P, D], F32R)
        pt0 = split("pt0", [P, 2 * P])
        yT = split("yT", [P, 2, KD, CH])
        keys = split("keys", [P, H // 2, 2 * J])
        v_main = sb("v_main", [P, H * DK])
        v_tail = split("v_tail", [P, G, PAIR])
        qT = split("qT", [P, 2, 2, CH])
        pt_main = sb("pt_main", [P, 2, HG, CH])
        pt_tail = split("pt_tail", [P, CH])
        cT = split("cT", [P, 2, 2, CH])
        y_rows = sb("y_rows", [P, 2, NT, D])
        acc = sb("acc", [P, NT, D])
        normed = sb("normed", [P, 2, 2, D])
        exps0 = sb("exps0", [P, 2, J])
        probs0 = sb("probs0", [P, 2, 2 * P])
        exps = sb("exps", [P, 2, HG, J])
        probs = sb("probs", [P, 2, HG * JP])
        ident = sb("ident", [P, P])
        mask = sb("mask", [P, 2, J])
        neg_max = sb("neg_max", [P, NT, HG])
        sums = sb("sums", [P, NT, HG])
        inv_sums = sb("inv_sums", [P, NT, HG])
        neg_max0 = sb("neg_max0", [P, 2])
        sums0 = sb("sums0", [P, 2])
        inv_sums0 = sb("inv_sums0", [P, 2])
        stats = sb("stats", [P, 2, 2, 6])
        mean_var = sb("mean_var", [P, 2, 2, 2])
        var_eps = sb("var_eps", [P, 2, 2])
        rstd = sb("rstd", [P, 2, 2])
        minus_half = sb("minus_half", [P, 2])

        wq_raw = pt_main[:, 0, :, :].rearrange("p h n -> p (h n)")
        wo_raw = pt_main[:, 1, :, :].rearrange("p h n -> p (h n)")
        wk0_raw = y_rows[:, 0, 0:2, :]
        wq0_raw = y_rows[:, 0, 2:4, :]
        wv0_raw = y_rows[:, 1, 0:2, :]
        wk0_s = [q[:, 0, 0, :].rearrange("p (k n) -> p k n", k=KD) for q in qT]
        wq0_s = [q[:, 0, 1, :].rearrange("p (k n) -> p k n", k=KD) for q in qT]

        def raw_tail(k):
            return ctx_raw[:, k, P:JP].unsqueeze(1).broadcast_to([P, HG, TR])

        score_bank = [es.enter_context(nc.psum_tensor(f"scores{n}", [P, 512], F32)) for n in range(BANKS)]
        job_bank = [es.enter_context(nc.psum_tensor(f"job{n}", [P, 512], F32)) for n in range(BANKS)]
        turned_main = es.enter_context(nc.psum_tensor("turned_main", [P, 512], F32))
        turned_tail = es.enter_context(nc.psum_tensor("turned_tail", [P, 512], F32))

        small_in = sem("small_in")
        ctx_in = sem("ctx_in")
        xT_in = sem("xT_in")
        x_rows_in = sem("x_rows_in")
        wkv_in = [sem("wkv_in0"), sem("wkv_in1")]
        wq_in = sem("wq_in")
        wo_in = sem("wo_in")
        affine_in = sem("affine_in")
        normed_free = [sem("normed_free0"), sem("normed_free1")]
        blanked = sem("blanked")
        zeroed = sem("zeroed")
        shaped = sem("shaped")
        setup_hi = sem("setup_hi")
        setup_lo = sem("setup_lo")
        ctx_hi = sem("ctx_hi")
        ctx_lo = sem("ctx_lo")
        x_hi = sem("x_hi")
        x_lo = sem("x_lo")
        wkv_hi = sem("wkv_hi")
        wkv_lo = sem("wkv_lo")
        filled = sem("filled")
        act_part = sem("act_part")
        emptied = sem("emptied")
        max0_ready = sem("max0_ready")
        inv0_ready = sem("inv0_ready")
        scores_ready = sem("scores_ready")
        masked = sem("masked")
        max_ready = sem("max_ready")
        exp_ready = sem("exp_ready")
        inv_ready = sem("inv_ready")
        probs_ready = sem("probs_ready")
        turned = sem("turned")
        main_out = sem("main_out")
        tail_hi = sem("tail_hi")
        tail_lo = sem("tail_lo")
        summed = sem("summed")
        stats_ready = sem("stats_ready")
        moments_ready = sem("moments_ready")
        var_ready = sem("var_ready")
        rstd_ready = sem("rstd_ready")
        centred = sem("centred")
        scaled = sem("scaled")
        shifted = sem("shifted")

        xT_v = xT.rearrange("(k p) (c n) -> c p k n", p=P, n=CH)
        x_v = x.rearrange("(c t p) d -> c p t d", p=P, t=NT)
        ctx_v = ctxT.rearrange("b (k p) j -> b p k j", p=P)
        wk_v = wk.rearrange("(k p) (g n) -> g p k n", p=P, n=D)
        wv_v = wv.rearrange("(k p) (g n) -> g p k n", p=P, n=D)
        out_v = out.rearrange("(u t p) d -> u p t d", p=P, t=2)

        block = es.enter_context(nc.Block())

        @block.sync
        def _(sp):
            def ahead(value):
                return value if isinstance(value, int) else sp.snap(value)

            def period(per):
                c, second = per.c, per.c % 2 == 1
                w = wk_v if second else wv_v
                loads_kv = per.next if second else per.own
                place = {}
                if per.next:
                    place["x"] = ahead(per.at(lambda c: c + 2) % NC)
                if second and per.next:
                    place["ctx"] = ahead(per.at(lambda c: (c + 1) // 2 + 1) % B)
                if c >= 1:
                    place["out"] = [ahead(per.at(lambda c: 2 * (c - 1) + half)) for half in range(2)]
                for s in range(NS):
                    if s == 0 and loads_kv:
                        for g in range(2):
                            if c >= 0:
                                sp.wait_ge(wkv_lo, per.at(lambda c: G * (c + 1) - 2 + g + 1))
                            sp.dma_start(wkv_raw[:, g, :, :], w[g]).then_inc(wkv_in[g], 16)
                    if s == CTX_STEP + 1 and second and per.next:
                        sp.wait_ge(ctx_lo, per.at(lambda c: (c + 1) // 2 + 1))
                        sp.dma_start(ctx_raw[:, :, 0:J], ctx_v[place["ctx"]]).then_inc(ctx_in, 16)
                    if s == X_STEP + 1 and per.next:
                        sp.wait_ge(x_lo, per.at(lambda c: c + 2))
                        sp.dma_start(xT_raw[:, :, :], xT_v[place["x"]]).then_inc(xT_in, 16)
                    if s == 11 and per.next:
                        sp.wait_ge(emptied, per.done(("attend0", c + 1, NT - 1)))
                        sp.dma_start(x_rows[:, :, :], x_v[place["x"]]).then_inc(x_rows_in, 16)
                    g = per.splits_weights(s)
                    if g is not None and g < 2:
                        sp.wait_ge(wkv_lo, per.at(lambda c: G * (c + 1) + g + 1))
                        sp.dma_start(wkv_raw[:, g, :, :], w[g + 2]).then_inc(wkv_in[g], 16)
                    for half in range(2):
                        if c >= 1 and s == NORM_STEPS[half] + 2:
                            sp.wait_ge(shifted, per.at(lambda c: 2 * (c - 1) + half + 1))
                            sp.dma_start(out_v[place["out"][half]],
                                         normed[:, half, :, :]).then_inc(normed_free[half], 16)
                    if c == -1 and s == 1:
                        sp.dma_start(wq_raw, wq.rearrange("(k p) n -> p k n", p=P)).then_inc(wq_in, 16)
                        sp.dma_start(wo_raw, wo.rearrange("(k p) n -> p k n", p=P)).then_inc(wo_in, 16)
                if c == -1:
                    sp.dma_start(gamma_b[:, :], gamma.partition_broadcast(P)).then_inc(affine_in, 16)
                    sp.dma_start(beta_b[:, :], beta.partition_broadcast(P)).then_inc(affine_in, 16)

            for dst, src in ((wk0_raw, wk0T), (wq0_raw, wq0T), (wv0_raw, wv0)):
                sp.dma_start(dst, src.rearrange("(k p) n -> p k n", p=P)).then_inc(small_in, 16)
            sp.wait_ge(zeroed, 1)
            sp.dma_start(ctx_raw[:, :, 0:J], ctx_v[0]).then_inc(ctx_in, 16)
            sp.dma_start(xT_raw[:, :, :], xT_v[0]).then_inc(xT_in, 16)
            sp.dma_start(x_rows[:, :, :], x_v[0]).then_inc(x_rows_in, 16)
            run_periods(sp, period)
            for half in range(2):
                sp.wait_ge(normed_free[half], 16 * NC + 1)
            sp.wait_ge(xT_in, 16 * (NC + 1))
            sp.wait_ge(x_rows_in, 16 * (NC + 1))
            sp.wait_ge(ctx_in, 16 * (B + 1))

        @block.gpsimd
        def _(pool):
            for half in range(2):
                pool.memset(normed[:, half, :, :], 0.0).then_inc(normed_free[half], 1)
            pool.memset(probs[:, :, :], 0.0).then_inc(blanked, 1)
            for blank in (*v_tail, *keys):
                pool.memset(blank[:, :, :].bitcast(F32), 0.0).then_inc(blanked, 1)
            pool.wait_ge(zeroed, 3)
            pool.affine_select(out=ident[:, :], in_=ident[:, :], compare_op=ALU.not_equal, fill=1.0,
                               base=0, pattern=[[-1, P]], channel_multiplier=1).then_inc(shaped, 1)
            for t in range(2):
                pool.affine_select(out=mask[:, t, :], in_=mask[:, t, :], compare_op=ALU.is_ge,
                                   fill=MASKED, base=t * P, pattern=[[-1, J]],
                                   channel_multiplier=1).then_inc(shaped, 1)

            def affine(per, half):
                k = per.at(lambda c: 2 * (c - 1) + half + 1)
                pool.wait_ge(centred, k)
                pool.tensor_tensor(normed[:, half, :, :], normed[:, half, :, :],
                                   gamma_b[:, :].unsqueeze(1).broadcast_to([P, 2, D]), ALU.mult)\
                    .then_inc(scaled, 1)
                pool.wait_ge(scaled, k)
                pool.tensor_tensor(normed[:, half, :, :], normed[:, half, :, :],
                                   beta_b[:, :].unsqueeze(1).broadcast_to([P, 2, D]), ALU.add)\
                    .then_inc(shifted, 1)

            def period(per):
                for s in range(NS):
                    at = per.summed(s)
                    if at:
                        c1, s1 = at
                        by = c1 - per.c
                        t = s1 % NT
                        pool.wait_ge(inv_ready, per.at(lambda c: NS * (c + by) + s1 + 1))
                        if c1 > 0 or s1 >= 2:
                            pool.wait_ge(turned, per.at(lambda c: NS * (c + by) + s1 - 1))
                        o = HG * P
                        for dst, first, keys_in in ((probs[:, s1 % 2, 0:o], 0, P), (probs[:, s1 % 2, o:], P, JT)):
                            dst = dst.rearrange("p (h j) -> p h j", h=HG)[:, :, 0:keys_in]
                            last = pool.tensor_tensor(
                                dst, exps[:, s1 % 2, :, first:first + keys_in],
                                inv_sums[:, t, :].unsqueeze(2).broadcast_to([P, HG, keys_in]), ALU.mult)
                        last.then_inc(probs_ready, 1)
                    for half in range(2):
                        if per.c >= 1 and s == NORM_STEPS[half]:
                            pool.wait_ge(var_ready, per.at(lambda c: 2 * (c - 1) + half + 1))
                            pool.tensor_tensor(rstd[:, half, :], var_eps[:, half, :], minus_half[:, :],
                                               ALU.pow).then_inc(rstd_ready, 1)
                        if per.c >= 1 and s == NORM_STEPS[half] + 1:
                            if per.c == 1 and half == 0:
                                pool.wait_ge(affine_in, 32)
                            affine(per, half)

            run_periods(pool, period)

        @block.scalar
        def _(act):
            def copy(dst, src, scale=1.0):
                return act.activation(dst, src, ACT.Copy, scale=scale)

            def job(per, job, bank):
                kind = job[0]
                if kind in BY_DVE_ALONE:
                    return
                if kind != "scores0":
                    act.wait_ge(filled, per.done(job))
                if kind == "fold0":
                    last = copy(fold[0][:, :, :], bank[:, :].rearrange("p (k n) -> p k n", k=KD), 1.0 / 16)
                elif kind == "mix0":
                    last = copy(mix[0][:, :, :], bank[:, 0:2 * JW].rearrange("p (k n) -> p k n", k=KD))
                elif kind == "values0":
                    copy(v0[0][:, :], bank[:, 0:D])
                    last = copy(v0_tail[0:TR, :], bank[0:TR, D:2 * D])
                elif kind == "scores0":
                    t = job[2]
                    act.wait_ge(max0_ready, per.at(lambda c: NT * (c + 1) + t + 1))
                    last = act.activation(exps0[:, t % 2, :], bank[:, 0:J], ACT.Exp,
                                          bias=neg_max0[:, t % 2:t % 2 + 1],
                                          accum_out=sums0[:, t % 2:t % 2 + 1])
                elif kind == "turn_p0":
                    last = copy(pt0[0][:, :], bank[:, 0:2 * P])
                elif kind == "turn_y":
                    t, par = job[2], job[1] % 2
                    last = copy(yT[0][:, par, :, t * P:(t + 1) * P],
                                bank[:, 0:2 * P].rearrange("p (k n) -> p k n", k=KD))
                elif kind == "queries":
                    last = copy(qT[0][:, job[2] % 2, job[3], :], bank[:, :])
                elif kind == "attend":
                    last = copy(cT[0][:, job[2] % 2, job[3], :], bank[:, :])
                elif kind == "values":
                    g = job[2]
                    copy(v_main[:, g * D:(g + 1) * D], bank[:, 0:D])
                    for q in range(HG):
                        o = (q % 2) * DK
                        last = copy(v_tail[0][q * TR:(q + 1) * TR, g, o:o + DK],
                                    bank[q * TR:(q + 1) * TR, D + q * DK:D + (q + 1) * DK])
                elif kind == "keys":
                    g = job[2]
                    src = bank[:, 0:2 * JW].rearrange("p (k n) -> p k n", k=2)
                    for a in range(2):
                        r = slice(a * DK, (a + 1) * DK)
                        last = copy(keys[0][r, 2 * g:2 * g + 2, a * J:(a + 1) * J], src[r, :, 0:J], 1.0 / 8)
                last.then_inc(act_part, 1)

            def jobs(per, s, place):
                for j in step_jobs(per.c, s)[place]:
                    job(per, j, job_bank[bank_of(j)])

            def period(per):
                for s in range(NS):
                    c, g, t = per.c, s // NT, s % NT
                    if c == -1 and s == 2:
                        act.wait_ge(blanked, BLANKED)
                    if c == -1 and s in (4, 12):
                        w, raw = (wq_s, wq_raw) if s == 4 else (wo_s, wo_raw)
                        act.wait_ge(wq_in if s == 4 else wo_in, 16)
                        copy(w[0][:, :, :].rearrange("p k n -> p (k n)"), raw).then_inc(setup_hi, 1)
                    w = per.splits_weights(s)
                    if w is not None:
                        if kv_job_before(c, w) in JOB:
                            act.wait_ge(filled, per.done(kv_job_before(c, w)))
                        act.wait_ge(wkv_in[w % 2], per.at(lambda c: 16 * (2 * (c + 1) + w // 2 + 1)))
                        copy(wkv[0][:, :, :], wkv_raw[:, w % 2, :, :]).then_inc(wkv_hi, 1)
                    if per.splits_ctx(s):
                        act.wait_ge(ctx_in, per.at(lambda c: 16 * ((c + 1) // 2 + 1)))
                        copy(ctx[0][:, :, :], ctx_raw[:, :, :])
                        for k in range(KD):
                            last = copy(ctx_tail[0][:, k, :, :], raw_tail(k))
                        last.then_inc(ctx_hi, 1)
                    if per.splits_x(s):
                        act.wait_ge(xT_in, per.at(lambda c: 16 * (c + 2)))
                        copy(xs[0][:, :, :], xT_raw[:, :, :]).then_inc(x_hi, 1)
                    jobs(per, s, "first")
                    if per.own:
                        act.wait_ge(turned, per.at(lambda c: NS * c + s + 1))
                        if c == 0 and s == 0:
                            act.wait_ge(setup_lo, 5)
                        if t == 0:
                            over = ("attend", c, g - 2, 1) if g >= 2 else ("attend", c - 1, g + 2, 1)
                            if over in JOB:
                                act.wait_ge(filled, per.done(over))
                        copy(pt_main[:, g % 2, :, t * P:(t + 1) * P],
                             turned_main[:, :].rearrange("p (h n) -> p h n", h=HG)).then_inc(main_out, 1)
                        if t == NT - 1:
                            over = ("attend", c, g - 1, 1) if g >= 1 else ("attend", c - 1, G - 1, 1)
                            if over in JOB:
                                act.wait_ge(filled, per.done(over))
                            copy(pt_tail[0][:, :], turned_tail[:, :]).then_inc(tail_hi, 1)
                    jobs(per, s, "mid")
                    if per.scored(s):
                        c1, s1 = per.scored(s)
                        by = c1 - c
                        t1 = s1 % NT
                        for pair in range(2):
                            u = 2 * s1 + pair
                            if pair == 0 and (c1 > 0 or s1 >= 2):
                                act.wait_ge(probs_ready, per.at(lambda c: NS * (c + by) + s1 - 1))
                            act.wait_ge(max_ready, per.at(lambda c: 2 * NS * (c + by) + u + 1))
                            for a in range(2):
                                h = 2 * pair + a
                                last = act.activation(
                                    exps[:, s1 % 2, h, :], score_bank[u % BANKS][:, a * J:(a + 1) * J],
                                    ACT.Exp, bias=neg_max[:, t1, h:h + 1], accum_out=sums[:, t1, h:h + 1])
                            last.then_inc(exp_ready, 1)
                    jobs(per, s, "last")

            act.wait_ge(small_in, 48)
            for dst, src in ((wk0_s[0], wk0_raw), (wq0_s[0], wq0_raw), (wv0_s[0][:, :, :], wv0_raw)):
                copy(dst, src).then_inc(setup_hi, 1)
            for j in SETUP_JOBS:
                job(Period(-1), j, job_bank[bank_of(j)])
            run_periods(act, period)

        @block.vector
        def _(dve):
            def lo(dst, whole, hi):
                return dve.tensor_tensor(dst, whole, hi.bitcast(F32), ALU.subtract)

            def lo_scaled(dst, whole, scale, hi):
                return dve.scalar_tensor_tensor(dst, whole, scale, hi.bitcast(F32), ALU.mult, ALU.subtract)

            def finish_scores0(per, s):
                for j in step_jobs(per.c, s)["mid"]:
                    if j[0] == "scores0":
                        t = j[2] % 2
                        dve.wait_ge(act_part, per.done_act(j))
                        dve.reciprocal(inv_sums0[:, t:t + 1], sums0[:, t:t + 1]).then_inc(inv0_ready, 1)
                        dve.wait_ge(inv0_ready, per.at(lambda c: NT * (c + 1) + j[2] + 1))
                        dve.tensor_scalar(probs0[:, t, 0:P], exps0[:, t, 0:P], inv_sums0[:, t:t + 1],
                                          None, ALU.mult)
                        dve.tensor_scalar(
                            probs0[:, t, P:].rearrange("p (r j) -> p r j", j=TR)[:, :, 0:JT],
                            exps0[:, t, P:J].unsqueeze(1).broadcast_to([P, P // TR, JT]),
                            inv_sums0[:, t:t + 1], None, ALU.mult).then_inc(emptied, 1)

            def job(per, job, bank):
                kind = job[0]
                if kind in BY_DVE_ALONE or kind == "scores0":
                    dve.wait_ge(filled, per.done(job))
                else:
                    dve.wait_ge(act_part, per.done_act(job))
                if kind == "fold0":
                    last = lo_scaled(fold[1][:, :, :].rearrange("p k n -> p (k n)"), bank[:, :], 1.0 / 16,
                                     fold[0][:, :, :].rearrange("p k n -> p (k n)"))
                elif kind == "mix0":
                    last = lo(mix[1][:, :, :].rearrange("p k n -> p (k n)"), bank[:, 0:2 * JW],
                              mix[0][:, :, :].rearrange("p k n -> p (k n)"))
                elif kind == "values0":
                    lo(v0[1][:, :], bank[:, 0:D], v0[0][:, :])
                    last = lo(v0_tail[TR:2 * TR, :], bank[0:TR, D:2 * D], v0_tail[0:TR, :])
                elif kind == "scores0":
                    t = job[2] % 2
                    dve.tensor_reduce(neg_max0[:, t:t + 1], bank[:, 0:J], AX.X, ALU.max, negate=True)\
                       .then_inc(max0_ready, 1)
                    return
                elif kind == "turn_p0":
                    last = lo(pt0[1][:, :], bank[:, 0:2 * P], pt0[0][:, :])
                elif kind == "attend0":
                    t, par = job[2], job[1] % 2
                    if t == 0:
                        dve.wait_ge(x_rows_in, per.at(lambda c: 16 * (c + 2)))
                    last = dve.tensor_tensor(y_rows[:, par, t, :], bank[:, 0:D], x_rows[:, t, :], ALU.add)
                elif kind == "turn_y":
                    t, par = job[2], job[1] % 2
                    cols = slice(t * P, (t + 1) * P)
                    last = lo(yT[1][:, par, :, cols], bank[:, 0:2 * P].rearrange("p (k n) -> p k n", k=KD),
                              yT[0][:, par, :, cols])
                elif kind == "queries":
                    g, pair = job[2] % 2, job[3]
                    last = lo(qT[1][:, g, pair, :], bank[:, :], qT[0][:, g, pair, :])
                elif kind == "attend":
                    g, pair = job[2] % 2, job[3]
                    last = lo(cT[1][:, g, pair, :], bank[:, :], cT[0][:, g, pair, :])
                elif kind == "values":
                    g = job[2]
                    for q in range(HG):
                        o = (q % 2) * DK
                        r = slice(q * TR, (q + 1) * TR)
                        last = lo(v_tail[1][r, g, o:o + DK], bank[q * TR:(q + 1) * TR, D + q * DK:D + (q + 1) * DK],
                                  v_tail[0][r, g, o:o + DK])
                elif kind == "keys":
                    g = job[2]
                    src = bank[:, 0:2 * JW].rearrange("p (k n) -> p k n", k=2)
                    for a in range(2):
                        r = slice(a * DK, (a + 1) * DK)
                        cols = slice(a * J, (a + 1) * J)
                        last = lo_scaled(keys[1][r, 2 * g:2 * g + 2, cols], src[r, :, 0:J], 1.0 / 8,
                                         keys[0][r, 2 * g:2 * g + 2, cols])
                elif kind == "project":
                    g, half = job[2], job[3]
                    two = slice(2 * half, 2 * half + 2)
                    base = y_rows[:, job[1] % 2, two, :] if g == 0 else acc[:, two, :]
                    last = dve.tensor_tensor(acc[:, two, :], bank[:, :].rearrange("p (t d) -> p t d", t=2),
                                             base, ALU.add)
                last.then_inc(emptied, 1)

            def tile_stats(per, half):
                dve.wait_ge(emptied, per.done(("project", per.c - 1, G - 1, half)))
                for t in range(2):
                    last = dve.bn_stats(stats[:, half, t, :], acc[:, 2 * half + t, :])
                last.then_inc(stats_ready, 1)

            def moments(per, half):
                for t in range(2):
                    last = dve.bn_aggr(mean_var[:, half, t, :], stats[:, half, t, :])
                last.then_inc(moments_ready, 1)
                dve.wait_ge(moments_ready, per.at(lambda c: 2 * (c - 1) + half + 1))
                dve.tensor_scalar(var_eps[:, half, :], mean_var[:, half, :, 1], EPS, None, ALU.add)\
                   .then_inc(var_ready, 1)

            def centre(per, half):
                dve.wait_ge(rstd_ready, per.at(lambda c: 2 * (c - 1) + half + 1))
                dve.wait_ge(normed_free[half], per.at(lambda c: 16 * (c - 1) + 1))
                for t in range(2):
                    last = dve.tensor_scalar(normed[:, half, t, :], acc[:, 2 * half + t, :],
                                             mean_var[:, half, t, 0:1], rstd[:, half, t:t + 1],
                                             ALU.subtract, ALU.mult)
                last.then_inc(centred, 1)

            def jobs(per, s, place):
                for j in step_jobs(per.c, s)[place]:
                    job(per, j, job_bank[bank_of(j)])

            def period(per):
                for s in range(NS):
                    c, g, t = per.c, s // NT, s % NT
                    if per.summed(s):
                        c1, s1 = per.summed(s)
                        by, t1 = c1 - c, s1 % NT
                        dve.wait_ge(exp_ready, per.at(lambda c: 2 * (NS * (c + by) + s1 + 1)))
                        dve.reciprocal(inv_sums[:, t1, :], sums[:, t1, :]).then_inc(inv_ready, 1)
                    if c == -1 and s == 2:
                        dve.wait_ge(blanked, BLANKED)
                    if c == -1 and s in (4, 12):
                        w, raw = (wq_s, wq_raw) if s == 4 else (wo_s, wo_raw)
                        dve.wait_ge(setup_hi, 4 if s == 4 else 5)
                        lo(w[1][:, :, :].rearrange("p k n -> p (k n)"), raw,
                           w[0][:, :, :].rearrange("p k n -> p (k n)")).then_inc(setup_lo, 1)
                    w = per.splits_weights(s)
                    if w is not None:
                        dve.wait_ge(wkv_hi, per.at(lambda c: G * (c + 1) + w + 1))
                        lo(wkv[1][:, :, :], wkv_raw[:, w % 2, :, :], wkv[0][:, :, :]).then_inc(wkv_lo, 1)
                    if per.splits_ctx(s):
                        dve.wait_ge(ctx_hi, per.at(lambda c: (c + 1) // 2 + 1))
                        lo(ctx[1][:, :, :], ctx_raw[:, :, :], ctx[0][:, :, :])
                        for k in range(KD):
                            last = lo(ctx_tail[1][:, k, :, :], raw_tail(k), ctx_tail[0][:, k, :, :])
                        last.then_inc(ctx_lo, 1)
                    if per.splits_x(s):
                        dve.wait_ge(x_hi, per.at(lambda c: c + 2))
                        lo(xs[1][:, :, :], xT_raw[:, :, :], xs[0][:, :, :]).then_inc(x_lo, 1)
                    for half in range(2):
                        if c >= 1 and s == NORM_STEPS[half]:
                            tile_stats(per, half)
                            dve.wait_ge(stats_ready, per.at(lambda c: 2 * (c - 1) + half + 1))
                    jobs(per, s, "first")
                    for half in range(2):
                        if c >= 1 and s == NORM_STEPS[half]:
                            moments(per, half)
                        if c >= 1 and s == NORM_STEPS[half] + 1:
                            centre(per, half)
                    if per.own and t == NT - 1:
                        dve.wait_ge(tail_hi, per.at(lambda c: G * c + g + 1))
                        lo(pt_tail[1][:, :], turned_tail[:, :], pt_tail[0][:, :]).then_inc(tail_lo, 1)
                    jobs(per, s, "mid")
                    if per.scored(s):
                        c1, s1 = per.scored(s)
                        by, t1 = c1 - c, s1 % NT
                        for pair in range(2):
                            u = 2 * s1 + pair
                            two = score_bank[u % BANKS][:, 0:2 * J].rearrange("p (h j) -> p h j", h=2)
                            dve.wait_ge(scores_ready, per.at(lambda c: 2 * NS * (c + by) + u + 1))
                            if c1 % 2 == 0 and t1 < 2:
                                if c1 == 0 and s1 == 0 and pair == 0:
                                    dve.wait_ge(shaped, 3)
                                dve.tensor_tensor(two, two, mask[:, t1, :].unsqueeze(1).broadcast_to([P, 2, J]),
                                                  ALU.add).then_inc(masked, 1)
                                dve.wait_ge(masked, per.at(
                                    lambda c: 4 * G * ((c + by) // 2) + 4 * (s1 // NT) + 2 * t1 + pair + 1))
                            dve.tensor_reduce(neg_max[:, t1, 2 * pair:2 * pair + 2], two, AX.X, ALU.max,
                                              negate=True).then_inc(max_ready, 1)
                    finish_scores0(per, s)
                    jobs(per, s, "last")

            dve.memset(ctx_raw[:, :, :], 0.0).then_inc(zeroed, 1)
            dve.memset(ident[:, :], 0.0).then_inc(zeroed, 1)
            dve.memset(mask[:, :, :], 0.0).then_inc(zeroed, 1)
            dve.memset(v0_tail[:, :].bitcast(F32), 0.0).then_inc(zeroed, 1)
            dve.memset(probs0[:, :, :], 0.0).then_inc(zeroed, 1)
            dve.memset(minus_half[:, :], -0.5).then_inc(zeroed, 1)
            for n, (dst, src, hi) in enumerate(((wk0_s[1], wk0_raw, wk0_s[0]), (wq0_s[1], wq0_raw, wq0_s[0]),
                                                (wv0_s[1][:, :, :], wv0_raw, wv0_s[0][:, :, :]))):
                dve.wait_ge(setup_hi, n + 1)
                lo(dst, src, hi).then_inc(setup_lo, 1)
            for j in SETUP_JOBS:
                job(Period(-1), j, job_bank[bank_of(j)])
            run_periods(dve, period)

        @block.tensor
        def _(pe):
            def product(dst, left, right, start=True, stop=True):
                n = len(left)
                for k in range(n):
                    (lh, ll), (rh, rl) = left[k], right[k]
                    for m, (a, b) in enumerate(((lh, rh), (lh, rl), (ll, rh))):
                        last = nc.tensor.matmul(dst, a, b, start=start and k == 0 and m == 0,
                                                stop=stop and k == n - 1 and m == 2,
                                                skip_group_check=not (start and stop))
                return last

            def tiles(pair, cols, *lead):
                return [tuple(part[(slice(None), *lead, k, cols)] for part in pair) for k in range(KD)]

            def job(per, job, bank):
                kind = job[0]
                if JOB[job] >= BANKS:
                    pe.wait_ge(emptied, per.at(lambda c: JOB[per.moved(job, c)] - BANKS + 1))
                if kind == "fold0":
                    pe.wait_ge(setup_lo, 2)
                    for k in range(KD):
                        last = product(bank[:, k * D:(k + 1) * D],
                                       [tuple(w[:, kk, k * P:(k + 1) * P] for w in wk0_s) for kk in range(KD)],
                                       [tuple(w[:, kk, :] for w in wq0_s) for kk in range(KD)])
                elif kind == "values0":
                    if per.c == -1:
                        pe.wait_ge(setup_lo, 3)
                    pe.wait_ge(ctx_lo, per.at(lambda c: (c + 1) // 2 + 1))
                    product(bank[:, 0:D], tiles(ctx, slice(0, P)), tiles(wv0_s, slice(0, D)))
                    last = product(bank[:, D:2 * D], [tuple(part[:, k, :, :].rearrange("p h j -> p (h j)") for part in ctx_tail) for k in range(KD)], tiles(wv0_s, slice(0, D)))
                elif kind == "mix0":
                    if per.c == -1:
                        pe.wait_ge(emptied, JOB[("fold0",)] + 1)
                    for k in range(KD):
                        last = product(bank[:, k * JW:(k + 1) * JW], tiles(fold, slice(k * P, (k + 1) * P)),
                                       tiles(ctx, slice(0, JW)))
                elif kind == "scores0":
                    t = job[2]
                    if t == 0:
                        pe.wait_ge(x_lo, per.at(lambda c: c + 2))
                        if job[1] % 2 == 0:
                            pe.wait_ge(emptied, per.done(("mix0", job[1] // 2)))
                    last = product(bank[:, 0:JW], tiles(xs, slice(t * P, (t + 1) * P)), tiles(mix, slice(0, JW)))
                elif kind == "turn_p0":
                    t = job[2]
                    pe.wait_ge(emptied, per.done(("scores0", job[1], t)))
                    if per.c == -1 and t == 0:
                        pe.wait_ge(shaped, 1)
                    nc.tensor.transpose(bank[:, 0:P], probs0[:, t % 2, 0:P], ident[:, :])
                    last = nc.tensor.transpose(bank[:, P:2 * P], probs0[:, t % 2, P:2 * P], ident[:, :])
                elif kind == "attend0":
                    pe.wait_ge(emptied, per.done(("turn_p0", job[1], job[2])))
                    dst = bank[:, 0:D]
                    product(dst, [(pt0[0][:, 0:P], pt0[1][:, 0:P])], [(v0[0][:, :], v0[1][:, :])], stop=False)
                    for part in range(2):
                        last = nc.tensor.matmul(dst, pt0[part][:, P:2 * P], v0_tail[:, :], start=False,
                                                stop=part == 1, skip_group_check=True)
                elif kind == "turn_y":
                    t, par = job[2], job[1] % 2
                    pe.wait_ge(emptied, per.done(("attend0", job[1], t)))
                    for k in range(KD):
                        last = nc.tensor.transpose(bank[:, k * P:(k + 1) * P],
                                                   y_rows[:, par, t, k * P:(k + 1) * P], ident[:, :])
                elif kind == "queries":
                    g, pair, par = job[2], job[3], job[1] % 2
                    if g == 0 and pair == 0:
                        if per.c == -1:
                            pe.wait_ge(setup_lo, 4)
                        pe.wait_ge(emptied, per.done(("turn_y", job[1], NT - 1)))
                    col = (2 * g + pair) * PAIR
                    last = product(bank[:, :], tiles(wq_s, slice(col, col + PAIR)),
                                   tiles(yT, slice(0, CH), par))
                elif kind in ("keys", "values"):
                    b, g = job[1], job[2]
                    pe.wait_ge(wkv_lo, per.at(lambda c: G * (c + 1) + g + 1))
                    if kind == "keys":
                        for pair in range(2):
                            last = product(bank[:, pair * JW:(pair + 1) * JW],
                                           tiles(wkv, slice(pair * PAIR, (pair + 1) * PAIR)),
                                           tiles(ctx, slice(0, JW)))
                    else:
                        product(bank[:, 0:D], tiles(ctx, slice(0, P)), tiles(wkv, slice(0, D)))
                        last = product(bank[:, D:2 * D], [tuple(part[:, k, :, :].rearrange("p h j -> p (h j)") for part in ctx_tail) for k in range(KD)], tiles(wkv, slice(0, D)))
                elif kind == "attend":
                    c, g, pair = job[1], job[2], job[3]
                    by = c - per.c
                    if pair == 0:
                        pe.wait_ge(main_out, per.at(lambda c: NS * (c + by) + NT * (g + 1)))
                        pe.wait_ge(tail_lo, per.at(lambda c: G * (c + by) + g + 1))
                        if c % 2 == 0:
                            pe.wait_ge(emptied, per.done(("values", c // 2, g)))
                    r = slice(pair * DK, (pair + 1) * DK)
                    product(bank[:, :], [(v_tail[0][r, g, :], v_tail[1][r, g, :])],
                            [(pt_tail[0][r, :], pt_tail[1][r, :])], stop=False)
                    for a in range(2):
                        h = 2 * pair + a
                        last = nc.tensor.matmul(bank[a * DK:(a + 1) * DK, :],
                                                v_main[:, (HG * g + h) * DK:(HG * g + h + 1) * DK],
                                                pt_main[:, g % 2, h, :], start=False, stop=True,
                                                skip_group_check=True)
                elif kind == "project":
                    c, g, half = job[1], job[2], job[3]
                    by = c - per.c
                    pe.wait_ge(emptied, per.done(("attend", c, g, 1)))
                    if c == 0 and g == 0 and half == 0:
                        pe.wait_ge(setup_lo, 5)
                    for t in range(2):
                        col = (2 * half + t) * P
                        last = product(bank[:, t * D:(t + 1) * D],
                                       [tuple(x[:, g % 2, pair, col:col + P] for x in cT) for pair in range(2)],
                                       [tuple(w[:, 2 * g + pair, :] for w in wo_s) for pair in range(2)])
                last.then_inc(filled, 1)

            def jobs(per, s, place):
                for j in step_jobs(per.c, s)[place]:
                    job(per, j, job_bank[bank_of(j)])

            def turn(per, s):
                g, t = s // NT, s % NT
                pe.wait_ge(probs_ready, per.at(lambda c: NS * c + s + 1))
                if per.c > 0 or s > 0:
                    pe.wait_ge(main_out, per.at(lambda c: NS * c + s))
                for h in range(HG):
                    nc.tensor.transpose(turned_main[:, h * P:(h + 1) * P], probs[:, s % 2, h * P:(h + 1) * P], ident[:, :])
                if t == 0 and (per.c > 0 or g > 0):
                    pe.wait_ge(tail_lo, per.at(lambda c: G * c + g))
                nc.tensor.transpose(turned_tail[:, t * P:(t + 1) * P], probs[:, s % 2, HG * P:], ident[:, :])\
                  .then_inc(turned, 1)

            def scores(per, s):
                c1, s1 = per.scored(s)
                by, g, t = c1 - per.c, s1 // NT, s1 % NT
                if t == 0:
                    pe.wait_ge(emptied, per.done(("queries", c1, g, 1)))
                    if c1 % 2 == 0:
                        pe.wait_ge(emptied, per.done(("keys", c1 // 2, g)))
                for pair in range(2):
                    u = 2 * s1 + pair
                    reuse = 2 if u < 2 else BANKS
                    if c1 > 0 or u >= BANKS:
                        pe.wait_ge(exp_ready, per.at(lambda c: 2 * NS * (c + by) + u - reuse + 1))
                    product(score_bank[u % BANKS][:, 0:2 * J],
                            [tuple(q[:, g % 2, pair, t * P:(t + 1) * P] for q in qT)],
                            [tuple(k[:, 2 * g + pair, :] for k in keys)]).then_inc(scores_ready, 1)

            def period(per):
                for s in range(NS):
                    jobs(per, s, "first")
                    if per.own:
                        turn(per, s)
                    jobs(per, s, "mid")
                    if per.scored(s):
                        scores(per, s)
                    jobs(per, s, "last")

            pe.wait_ge(zeroed, ZEROED)
            for j in SETUP_JOBS:
                job(Period(-1), j, job_bank[bank_of(j)])
            run_periods(pe, period)


_NAMES = ("xT", "x", "ctxT", "wq0T", "wk0T", "wv0", "wq", "wk", "wv", "wo", "gamma", "beta")


def kernel(**inputs):
    import numpy as np
    import concourse.bacc as bacc
    from concourse.bass_utils import run_bass_kernel_spmd

    x = np.asarray(inputs["x"]).reshape(B * S, D)
    layouts = {
        "xT": x.T, "x": x, "ctxT": np.asarray(inputs["ctx_1024"]).transpose(0, 2, 1),
        "wq0T": np.asarray(inputs["L0_xattn_Wq"]).T, "wk0T": np.asarray(inputs["L0_xattn_Wk"]).T,
        "wv0": inputs["L0_xattn_Wv"], "wq": inputs["L1_xattn_W_Q"], "wk": inputs["L1_xattn_W_K"],
        "wv": inputs["L1_xattn_W_V"], "wo": inputs["L1_xattn_W_O"],
        "gamma": inputs["L1_xattn_ln_gamma"], "beta": inputs["L1_xattn_ln_beta"],
    }
    nc = bacc.Bacc("TRN2", target_bir_lowering=False, num_devices=1)
    arrays, args = {}, []
    for name in _NAMES:
        a = np.ascontiguousarray(layouts[name])
        arrays[name + "_dram"] = a
        args.append(nc.dram_tensor(name + "_dram", a.shape, mybir.dt.from_np(a.dtype), kind="ExternalInput").ap())
    args.append(nc.dram_tensor("out_dram", (B * S, D), F32, kind="ExternalOutput").ap())
    cross_attention(nc, *args)
    r = run_bass_kernel_spmd(nc, [arrays], core_ids=[0])
    return r.results[0]["out_dram"].reshape(B, S, D)
```

```python
import concourse.bass as bass
from concourse import mybir
from contextlib import ExitStack

F32 = mybir.dt.float32
F32R = mybir.dt.float32r
ALU = mybir.AluOpType
ACT = mybir.ActivationFunctionType
AX = mybir.AxisListType

P = 128
B, S, J, D = 4, 1024, 154, 256
H, DK = 16, 64
KD = D // P
JT = J - P
TR = 32
JP = P + TR
JW = 192
CH = 512
NT = CH // P
NC = B * S // CH
G = 4
HG = H // G
NS = G * NT
PAIR = 2 * DK
EPS = 1e-5
MASKED = -1.0e9
ZEROED, BLANKED = 6, 5
BANKS = 3


PLACES = ("first", "mid", "last")
SCHEDULE = {
    "project": ((8, "last"), (9, "last"), (12, "last"), (14, "last"),
                (16, "last"), (17, "last"), (20, "last"), (21, "last")),
    "queries": ((-4, "first"), (-4, "first"), (-2, "first"), (-1, "last"),
                (3, "last"), (4, "first"), (6, "first"), (8, "first")),
    "mix0": ((-16, "mid"),),
    "values0": ((-15, "last"),),
    "turn_y": ((-12, "last"), (-10, "mid"), (-8, "mid"), (-6, "mid")),
    "attend0": ((-13, "mid"), (-11, "mid"), (-9, "first"), (-7, "mid")),
    "turn_p0": ((-14, "first"), (-13, "mid"), (-10, "mid"), (-8, "mid")),
    "scores0": ((-15, "mid"), (-14, "mid"), (-11, "mid"), (-9, "mid")),
    "attend": ((5, "first"), (7, "first"), (9, "first"), (11, "first"),
               (14, "first"), (15, "first"), (17, "first"), (19, "first")),
    "keys": ((-14, "last"), (-10, "last"), (-6, "last"), (-1, "last")),
    "values": ((3, "last"), (6, "last"), (10, "last"), (14, "first")),
}
START = {
    "mix0": ((-16, "last"),),
    "values0": ((-15, "first"),),
    "turn_y": ((-12, "mid"), (-11, "mid"), (-10, "mid"), (-10, "last")),
    "attend0": ((-13, "mid"), (-12, "mid"), (-11, "mid"), (-10, "mid")),
    "turn_p0": ((-14, "mid"), (-13, "mid"), (-12, "mid"), (-11, "mid")),
    "scores0": ((-15, "mid"), (-14, "mid"), (-13, "mid"), (-12, "mid")),
    "queries": ((-7, "first"), (-5, "last"), (-2, "first")),
    "keys": ((-14, "last"), (-10, "last"), (-6, "last"), (-2, "last")),
}
BY_BATCH = ("mix0", "values0", "keys", "values")
BY_TWO = ("attend", "queries", "project")
CTX_STEP, X_STEP = 15, 0
WEIGHT_STEPS = (4, 11)
NORM_STEPS = (5, 6)


def step_jobs(c, s):
    at = {place: [] for place in PLACES}
    for kind, entries in SCHEDULE.items():
        for n, (when, place) in enumerate(entries):
            if c == -1:
                when, place = START[kind][n] if n < len(START.get(kind, ())) else (when, place)
            chunk, r = divmod(NS * c + s - when, NS)
            if r or not 0 <= chunk < NC or kind in BY_BATCH and chunk % 2:
                continue
            if kind in BY_BATCH:
                index = (chunk // 2,) + ((n,) if len(entries) > 1 else ())
            else:
                index = (chunk,) + (divmod(n, 2) if kind in BY_TWO else (n,))
            at[place].append((kind,) + index)
    return at


def kv_job_in(c, s):
    for jobs in step_jobs(c, s).values():
        for job in jobs:
            if job[0] in ("keys", "values"):
                return job[2]
    return None


SETUP_JOBS = [("fold0",)]
BY_DVE_ALONE = ("attend0", "project")


def number_jobs():
    order = list(SETUP_JOBS)
    for c in range(-1, NC + 1):
        for s in range(NS):
            at = step_jobs(c, s)
            order += [job for place in PLACES for job in at[place]]
    return ({job: k for k, job in enumerate(order)},
            {job: k for k, job in enumerate(j for j in order if j[0] not in BY_DVE_ALONE)})


JOB, ACT_JOB = number_jobs()


def bank_of(job):
    return JOB[job] % BANKS


class Period:

    def __init__(self, c0, i=None):
        self.c, self.i = c0, i

    def at(self, count):
        base = count(self.c)
        if self.i is None:
            return base
        rise = count(self.c + 2) - base
        assert count(self.c + 4) == base + 2 * rise
        return base + self.i * rise if rise else base

    def moved(self, job, c):
        by = c - self.c
        if not by:
            return job
        if job[0] in ("keys", "values", "values0", "mix0"):
            by //= 2
        return (job[0], job[1] + by) + job[2:]

    def done(self, job):
        return self.at(lambda c: JOB[self.moved(job, c)] + 1)

    def done_act(self, job):
        return self.at(lambda c: ACT_JOB[self.moved(job, c)] + 1)

    @property
    def own(self):
        return 0 <= self.c < NC

    @property
    def next(self):
        return -1 <= self.c < NC - 1

    def scored(self, s):
        if s + 2 < NS:
            return (self.c, s + 2) if self.own else None
        return (self.c + 1, s + 2 - NS) if self.next else None

    def summed(self, s):
        if s + 1 < NS:
            return (self.c, s + 1) if self.own else None
        return (self.c + 1, s + 1 - NS) if self.next else None

    def splits_weights(self, s):
        return kv_job_in(self.c, s + 1) if s + 1 < NS else None

    def splits_ctx(self, s):
        return s == CTX_STEP and self.c % 2 == 0 and self.own

    def splits_x(self, s):
        return s == X_STEP and self.next and self.c >= 0


def kv_job_before(c, w):
    b = c // 2
    if c % 2 == 1:
        return ("keys", b + 1, w - 1) if w else ("values", b, G - 1)
    return ("values", b, w - 1) if w else ("keys", b, G - 1)


def run_periods(engine, period):
    period(Period(-1))
    period(Period(0))
    with engine.Fori(0, (NC - 2) // 2) as i:
        period(Period(1, i))
        period(Period(2, i))
    period(Period(NC - 1))
    period(Period(NC))


def cross_attention(nc, xT, x, ctxT, wq0T, wk0T, wv0, wq, wk, wv, wo, gamma, beta, out):
    es = ExitStack()
    with es:
        def sb(name, shape, dt=F32):
            return es.enter_context(nc.sbuf_tensor(name, shape, dt))

        def sem(name):
            return es.enter_context(nc.semaphore(name))

        def split(name, shape):
            return sb(name + "_hi", shape, F32R), sb(name + "_lo", shape, F32R)

        xT_raw = sb("xT_raw", [P, KD, CH])
        x_rows = sb("x_rows", [P, NT, D])
        ctx_raw = sb("ctx_raw", [P, KD, JW])
        wkv_raw = sb("wkv_raw", [P, 2, KD, D])
        gamma_b = sb("gamma_b", [P, D])
        beta_b = sb("beta_b", [P, D])
        xs = split("xs", [P, KD, CH])
        ctx = split("ctx", [P, KD, JW])
        ctx_tail = split("ctx_tail", [P, KD, HG, TR])
        wkv = split("wkv", [P, KD, D])
        wq_s = split("wq", [P, KD, H * DK])
        wo_s = split("wo", [P, H * DK // P, D])
        wv0_s = split("wv0", [P, KD, D])
        fold = split("fold", [P, KD, D])
        mix = split("mix", [P, KD, JW])
        v0 = split("v0", [P, D])
        v0_tail = sb("v0_tail", [P, D], F32R)
        pt0 = split("pt0", [P, 2 * P])
        yT = split("yT", [P, 2, KD, CH])
        keys = split("keys", [P, H // 2, 2 * J])
        v_main = sb("v_main", [P, H * DK])
        v_tail = split("v_tail", [P, G, PAIR])
        qT = split("qT", [P, 2, 2, CH])
        pt_main = sb("pt_main", [P, 2, HG, CH])
        pt_tail = split("pt_tail", [P, CH])
        cT = split("cT", [P, 2, 2, CH])
        y_rows = sb("y_rows", [P, 2, NT, D])
        acc = sb("acc", [P, NT, D])
        normed = sb("normed", [P, 2, 2, D])
        exps0 = sb("exps0", [P, 2, J])
        probs0 = sb("probs0", [P, 2, 2 * P])
        exps = sb("exps", [P, 2, HG, J])
        probs = sb("probs", [P, 2, HG * JP])
        ident = sb("ident", [P, P])
        mask = sb("mask", [P, 2, J])
        neg_max = sb("neg_max", [P, NT, HG])
        sums = sb("sums", [P, NT, HG])
        inv_sums = sb("inv_sums", [P, NT, HG])
        neg_max0 = sb("neg_max0", [P, 2])
        sums0 = sb("sums0", [P, 2])
        inv_sums0 = sb("inv_sums0", [P, 2])
        stats = sb("stats", [P, 2, 2, 6])
        mean_var = sb("mean_var", [P, 2, 2, 2])
        var_eps = sb("var_eps", [P, 2, 2])
        rstd = sb("rstd", [P, 2, 2])
        minus_half = sb("minus_half", [P, 2])

        wq_raw = pt_main[:, 0, :, :].rearrange("p h n -> p (h n)")
        wo_raw = pt_main[:, 1, :, :].rearrange("p h n -> p (h n)")
        wk0_raw = y_rows[:, 0, 0:2, :]
        wq0_raw = y_rows[:, 0, 2:4, :]
        wv0_raw = y_rows[:, 1, 0:2, :]
        wk0_s = [q[:, 0, 0, :].rearrange("p (k n) -> p k n", k=KD) for q in qT]
        wq0_s = [q[:, 0, 1, :].rearrange("p (k n) -> p k n", k=KD) for q in qT]

        def raw_tail(k):
            return ctx_raw[:, k, P:JP].unsqueeze(1).broadcast_to([P, HG, TR])

        score_bank = [es.enter_context(nc.psum_tensor(f"scores{n}", [P, 512], F32)) for n in range(BANKS)]
        job_bank = [es.enter_context(nc.psum_tensor(f"job{n}", [P, 512], F32)) for n in range(BANKS)]
        turned_main = es.enter_context(nc.psum_tensor("turned_main", [P, 512], F32))
        turned_tail = es.enter_context(nc.psum_tensor("turned_tail", [P, 512], F32))

        small_in = [sem("wk0_in"), sem("wq0_in"), sem("wv0_in")]
        ctx_in = sem("ctx_in")
        xT_in = sem("xT_in")
        x_rows_in = sem("x_rows_in")
        wkv_in = [sem("wkv_in0"), sem("wkv_in1")]
        wq_in = sem("wq_in")
        wo_in = sem("wo_in")
        affine_in = sem("affine_in")
        normed_free = [sem("normed_free0"), sem("normed_free1")]
        blanked = sem("blanked")
        zeroed = sem("zeroed")
        shaped = sem("shaped")
        setup_hi = sem("setup_hi")
        setup_lo = sem("setup_lo")
        ctx_hi = sem("ctx_hi")
        ctx_lo = sem("ctx_lo")
        x_hi = sem("x_hi")
        x_lo = sem("x_lo")
        wkv_hi = sem("wkv_hi")
        wkv_lo = sem("wkv_lo")
        filled = sem("filled")
        act_part = sem("act_part")
        emptied = sem("emptied")
        max0_ready = sem("max0_ready")
        inv0_ready = sem("inv0_ready")
        scores_ready = sem("scores_ready")
        masked = sem("masked")
        max_ready = sem("max_ready")
        exp_ready = sem("exp_ready")
        inv_ready = sem("inv_ready")
        probs_ready = sem("probs_ready")
        turned = sem("turned")
        main_out = sem("main_out")
        tail_hi = sem("tail_hi")
        tail_lo = sem("tail_lo")
        stats_ready = sem("stats_ready")
        moments_ready = sem("moments_ready")
        var_ready = sem("var_ready")
        rstd_ready = sem("rstd_ready")
        centred = sem("centred")
        scaled = sem("scaled")
        shifted = sem("shifted")

        xT_v = xT.rearrange("(k p) (c n) -> c p k n", p=P, n=CH)
        x_v = x.rearrange("(c t p) d -> c p t d", p=P, t=NT)
        ctx_v = ctxT.rearrange("b (k p) j -> b p k j", p=P)
        wk_v = wk.rearrange("(k p) (g n) -> g p k n", p=P, n=D)
        wv_v = wv.rearrange("(k p) (g n) -> g p k n", p=P, n=D)
        out_v = out.rearrange("(u t p) d -> u p t d", p=P, t=2)

        block = es.enter_context(nc.Block())

        @block.sync
        def _(sp):
            def ahead(value):
                return value if isinstance(value, int) else sp.snap(value)

            def period(per):
                c, second = per.c, per.c % 2 == 1
                w = wk_v if second else wv_v
                loads_kv = per.next if second else per.own
                place = {}
                if per.next:
                    place["x"] = ahead(per.at(lambda c: c + 2) % NC)
                if second and per.next:
                    place["ctx"] = ahead(per.at(lambda c: (c + 1) // 2 + 1) % B)
                if c >= 1:
                    place["out"] = [ahead(per.at(lambda c: 2 * (c - 1) + half)) for half in range(2)]
                for s in range(NS):
                    if s == 0 and loads_kv:
                        for g in range(2):
                            if c >= 0:
                                sp.wait_ge(wkv_lo, per.at(lambda c: G * (c + 1) - 2 + g + 1))
                            sp.dma_start(wkv_raw[:, g, :, :], w[g]).then_inc(wkv_in[g], 16)
                    if c == -1 and s == 0:
                        sp.dma_start(wq_raw, wq.rearrange("(k p) n -> p k n", p=P)).then_inc(wq_in, 16)
                        sp.dma_start(wo_raw, wo.rearrange("(k p) n -> p k n", p=P)).then_inc(wo_in, 16)
                    if s == 1 and second and per.next:
                        sp.wait_ge(ctx_lo, per.at(lambda c: (c + 1) // 2 + 1))
                        sp.dma_start(ctx_raw[:, :, 0:J], ctx_v[place["ctx"]]).then_inc(ctx_in, 16)
                    if s == X_STEP + 1 and per.next:
                        sp.wait_ge(x_lo, per.at(lambda c: c + 2))
                        sp.dma_start(xT_raw[:, :, :], xT_v[place["x"]]).then_inc(xT_in, 16)
                    if s == 11 and per.next:
                        sp.wait_ge(emptied, per.done(("attend0", c + 1, NT - 1)))
                        sp.dma_start(x_rows[:, :, :], x_v[place["x"]]).then_inc(x_rows_in, 16)
                    g = per.splits_weights(s)
                    if g is not None and g < 2:
                        sp.wait_ge(wkv_lo, per.at(lambda c: G * (c + 1) + g + 1))
                        sp.dma_start(wkv_raw[:, g, :, :], w[g + 2]).then_inc(wkv_in[g], 16)
                    for half in range(2):
                        if c >= 1 and s == NORM_STEPS[half] + 2:
                            sp.wait_ge(shifted, per.at(lambda c: 2 * (c - 1) + half + 1))
                            sp.dma_start(out_v[place["out"][half]],
                                         normed[:, half, :, :]).then_inc(normed_free[half], 16)
                if c == -1:
                    sp.dma_start(gamma_b[:, :], gamma.partition_broadcast(P)).then_inc(affine_in, 16)
                    sp.dma_start(beta_b[:, :], beta.partition_broadcast(P)).then_inc(affine_in, 16)

            for n, (dst, src) in enumerate(((wk0_raw, wk0T), (wq0_raw, wq0T), (wv0_raw, wv0))):
                sp.dma_start(dst, src.rearrange("(k p) n -> p k n", p=P)).then_inc(small_in[n], 16)
                if n == 1:
                    sp.wait_ge(zeroed, 1)
                    sp.dma_start(ctx_raw[:, :, 0:J], ctx_v[0]).then_inc(ctx_in, 16)
            sp.dma_start(xT_raw[:, :, :], xT_v[0]).then_inc(xT_in, 16)
            sp.dma_start(x_rows[:, :, :], x_v[0]).then_inc(x_rows_in, 16)
            run_periods(sp, period)
            for half in range(2):
                sp.wait_ge(normed_free[half], 16 * NC + 1)
            sp.wait_ge(xT_in, 16 * (NC + 1))
            sp.wait_ge(x_rows_in, 16 * (NC + 1))
            sp.wait_ge(ctx_in, 16 * (B + 1))

        @block.gpsimd
        def _(pool):
            for half in range(2):
                pool.memset(normed[:, half, :, :], 0.0).then_inc(normed_free[half], 1)
            pool.memset(probs[:, :, :], 0.0).then_inc(blanked, 1)
            for blank in (*v_tail, *keys):
                pool.memset(blank[:, :, :].bitcast(F32), 0.0).then_inc(blanked, 1)
            pool.wait_ge(zeroed, 3)
            pool.affine_select(out=ident[:, :], in_=ident[:, :], compare_op=ALU.not_equal, fill=1.0,
                               base=0, pattern=[[-1, P]], channel_multiplier=1).then_inc(shaped, 1)
            for t in range(2):
                pool.affine_select(out=mask[:, t, :], in_=mask[:, t, :], compare_op=ALU.is_ge,
                                   fill=MASKED, base=t * P, pattern=[[-1, J]],
                                   channel_multiplier=1).then_inc(shaped, 1)

            def affine(per, half):
                k = per.at(lambda c: 2 * (c - 1) + half + 1)
                pool.wait_ge(centred, k)
                pool.tensor_tensor(normed[:, half, :, :], normed[:, half, :, :],
                                   gamma_b[:, :].unsqueeze(1).broadcast_to([P, 2, D]), ALU.mult)\
                    .then_inc(scaled, 1)
                pool.wait_ge(scaled, k)
                pool.tensor_tensor(normed[:, half, :, :], normed[:, half, :, :],
                                   beta_b[:, :].unsqueeze(1).broadcast_to([P, 2, D]), ALU.add)\
                    .then_inc(shifted, 1)

            def period(per):
                for s in range(NS):
                    at = per.summed(s)
                    if at:
                        c1, s1 = at
                        by = c1 - per.c
                        t = s1 % NT
                        pool.wait_ge(inv_ready, per.at(lambda c: NS * (c + by) + s1 + 1))
                        if c1 > 0 or s1 >= 2:
                            pool.wait_ge(turned, per.at(lambda c: NS * (c + by) + s1 - 1))
                        o = HG * P
                        for dst, first, keys_in in ((probs[:, s1 % 2, 0:o], 0, P), (probs[:, s1 % 2, o:], P, JT)):
                            dst = dst.rearrange("p (h j) -> p h j", h=HG)[:, :, 0:keys_in]
                            last = pool.tensor_tensor(
                                dst, exps[:, s1 % 2, :, first:first + keys_in],
                                inv_sums[:, t, :].unsqueeze(2).broadcast_to([P, HG, keys_in]), ALU.mult)
                        last.then_inc(probs_ready, 1)
                    for half in range(2):
                        if per.c >= 1 and s == NORM_STEPS[half]:
                            pool.wait_ge(var_ready, per.at(lambda c: 2 * (c - 1) + half + 1))
                            pool.tensor_tensor(rstd[:, half, :], var_eps[:, half, :], minus_half[:, :],
                                               ALU.pow).then_inc(rstd_ready, 1)
                        if per.c >= 1 and s == NORM_STEPS[half] + 1:
                            if per.c == 1 and half == 0:
                                pool.wait_ge(affine_in, 32)
                            affine(per, half)

            run_periods(pool, period)

        @block.scalar
        def _(act):
            def copy(dst, src, scale=1.0):
                return act.activation(dst, src, ACT.Copy, scale=scale)

            def job(per, job, bank):
                kind = job[0]
                if kind in BY_DVE_ALONE:
                    return
                if kind != "scores0":
                    act.wait_ge(filled, per.done(job))
                if kind == "fold0":
                    last = copy(fold[0][:, :, :], bank[:, :].rearrange("p (k n) -> p k n", k=KD), 1.0 / 16)
                elif kind == "mix0":
                    last = copy(mix[0][:, :, :], bank[:, 0:2 * JW].rearrange("p (k n) -> p k n", k=KD))
                elif kind == "values0":
                    copy(v0[0][:, :], bank[:, 0:D])
                    last = copy(v0_tail[0:TR, :], bank[0:TR, D:2 * D])
                elif kind == "scores0":
                    t = job[2]
                    act.wait_ge(max0_ready, per.at(lambda c: NT * (c + 1) + t + 1))
                    last = act.activation(exps0[:, t % 2, :], bank[:, 0:J], ACT.Exp,
                                          bias=neg_max0[:, t % 2:t % 2 + 1],
                                          accum_out=sums0[:, t % 2:t % 2 + 1])
                elif kind == "turn_p0":
                    last = copy(pt0[0][:, :], bank[:, 0:2 * P])
                elif kind == "turn_y":
                    t, par = job[2], job[1] % 2
                    last = copy(yT[0][:, par, :, t * P:(t + 1) * P],
                                bank[:, 0:2 * P].rearrange("p (k n) -> p k n", k=KD))
                elif kind == "queries":
                    last = copy(qT[0][:, job[2] % 2, job[3], :], bank[:, :])
                elif kind == "attend":
                    last = copy(cT[0][:, job[2] % 2, job[3], :], bank[:, :])
                elif kind == "values":
                    g = job[2]
                    copy(v_main[:, g * D:(g + 1) * D], bank[:, 0:D])
                    for q in range(HG):
                        o = (q % 2) * DK
                        last = copy(v_tail[0][q * TR:(q + 1) * TR, g, o:o + DK],
                                    bank[q * TR:(q + 1) * TR, D + q * DK:D + (q + 1) * DK])
                elif kind == "keys":
                    g = job[2]
                    src = bank[:, 0:2 * JW].rearrange("p (k n) -> p k n", k=2)
                    for a in range(2):
                        r = slice(a * DK, (a + 1) * DK)
                        last = copy(keys[0][r, 2 * g:2 * g + 2, a * J:(a + 1) * J], src[r, :, 0:J], 1.0 / 8)
                last.then_inc(act_part, 1)

            def split_ctx(per):
                act.wait_ge(ctx_in, per.at(lambda c: 16 * ((c + 2) // 2 + 1)))
                copy(ctx[0][:, :, :], ctx_raw[:, :, :])
                for k in range(KD):
                    last = copy(ctx_tail[0][:, k, :, :], raw_tail(k))
                last.then_inc(ctx_hi, 1)

            def split_x(per):
                act.wait_ge(xT_in, per.at(lambda c: 16 * (c + 2)))
                copy(xs[0][:, :, :], xT_raw[:, :, :]).then_inc(x_hi, 1)

            def jobs(per, s, place):
                for j in step_jobs(per.c, s)[place]:
                    job(per, j, job_bank[bank_of(j)])

            def period(per):
                for s in range(NS):
                    c, g, t = per.c, s // NT, s % NT
                    if c == -1 and s == 1:
                        act.wait_ge(blanked, BLANKED)
                    for n, (w, raw) in enumerate(((wq_s, wq_raw), (wo_s, wo_raw))):
                        if c != -1 or s != WEIGHT_STEPS[n]:
                            continue
                        act.wait_ge((wq_in, wo_in)[n], 16)
                        copy(w[0][:, :, :].rearrange("p k n -> p (k n)"), raw).then_inc(setup_hi, 1)
                    if per.splits_ctx(s):
                        split_ctx(per)
                    if per.splits_x(s):
                        split_x(per)
                    w = per.splits_weights(s)
                    if w is not None:
                        if kv_job_before(c, w) in JOB:
                            act.wait_ge(filled, per.done(kv_job_before(c, w)))
                        act.wait_ge(wkv_in[w % 2], per.at(lambda c: 16 * (2 * (c + 1) + w // 2 + 1)))
                        copy(wkv[0][:, :, :], wkv_raw[:, w % 2, :, :]).then_inc(wkv_hi, 1)
                    jobs(per, s, "first")
                    if per.own:
                        act.wait_ge(turned, per.at(lambda c: NS * c + s + 1))
                        if c == 0 and s == 0:
                            act.wait_ge(setup_lo, 5)
                        if t == 0:
                            over = ("attend", c, g - 2, 1) if g >= 2 else ("attend", c - 1, g + 2, 1)
                            if over in JOB:
                                act.wait_ge(filled, per.done(over))
                        copy(pt_main[:, g % 2, :, t * P:(t + 1) * P],
                             turned_main[:, :].rearrange("p (h n) -> p h n", h=HG)).then_inc(main_out, 1)
                        if t == NT - 1:
                            over = ("attend", c, g - 1, 1) if g >= 1 else ("attend", c - 1, G - 1, 1)
                            if over in JOB:
                                act.wait_ge(filled, per.done(over))
                            copy(pt_tail[0][:, :], turned_tail[:, :]).then_inc(tail_hi, 1)
                    jobs(per, s, "mid")
                    if per.scored(s):
                        c1, s1 = per.scored(s)
                        by = c1 - c
                        t1 = s1 % NT
                        for pair in range(2):
                            u = 2 * s1 + pair
                            if pair == 0 and (c1 > 0 or s1 >= 2):
                                act.wait_ge(probs_ready, per.at(lambda c: NS * (c + by) + s1 - 1))
                            act.wait_ge(max_ready, per.at(lambda c: 2 * NS * (c + by) + u + 1))
                            for a in range(2):
                                h = 2 * pair + a
                                last = act.activation(
                                    exps[:, s1 % 2, h, :], score_bank[u % BANKS][:, a * J:(a + 1) * J],
                                    ACT.Exp, bias=neg_max[:, t1, h:h + 1], accum_out=sums[:, t1, h:h + 1])
                            last.then_inc(exp_ready, 1)
                    jobs(per, s, "last")

            for n, (dst, src) in enumerate(((wk0_s[0], wk0_raw), (wq0_s[0], wq0_raw), (wv0_s[0][:, :, :], wv0_raw))):
                act.wait_ge(small_in[n], 16)
                copy(dst, src).then_inc(setup_hi, 1)
                if n == 1:
                    split_ctx(Period(-1))
            split_x(Period(-1))
            for j in SETUP_JOBS:
                job(Period(-1), j, job_bank[bank_of(j)])
            run_periods(act, period)

        @block.vector
        def _(dve):
            def lo(dst, whole, hi):
                return dve.tensor_tensor(dst, whole, hi.bitcast(F32), ALU.subtract)

            def lo_scaled(dst, whole, scale, hi):
                return dve.scalar_tensor_tensor(dst, whole, scale, hi.bitcast(F32), ALU.mult, ALU.subtract)

            def finish_scores0(per, s):
                at = step_jobs(per.c, s)
                for j in at["first"] + at["mid"]:
                    if j[0] == "scores0":
                        t = j[2] % 2
                        dve.wait_ge(act_part, per.done_act(j))
                        dve.reciprocal(inv_sums0[:, t:t + 1], sums0[:, t:t + 1]).then_inc(inv0_ready, 1)
                        dve.wait_ge(inv0_ready, per.at(lambda c: NT * (c + 1) + j[2] + 1))
                        dve.tensor_scalar(probs0[:, t, 0:P], exps0[:, t, 0:P], inv_sums0[:, t:t + 1],
                                          None, ALU.mult)
                        dve.tensor_scalar(
                            probs0[:, t, P:].rearrange("p (r j) -> p r j", j=TR)[:, :, 0:JT],
                            exps0[:, t, P:J].unsqueeze(1).broadcast_to([P, P // TR, JT]),
                            inv_sums0[:, t:t + 1], None, ALU.mult).then_inc(emptied, 1)

            def job(per, job, bank):
                kind = job[0]
                if kind in BY_DVE_ALONE or kind == "scores0":
                    dve.wait_ge(filled, per.done(job))
                else:
                    dve.wait_ge(act_part, per.done_act(job))
                if kind == "fold0":
                    last = lo_scaled(fold[1][:, :, :].rearrange("p k n -> p (k n)"), bank[:, :], 1.0 / 16,
                                     fold[0][:, :, :].rearrange("p k n -> p (k n)"))
                elif kind == "mix0":
                    last = lo(mix[1][:, :, :].rearrange("p k n -> p (k n)"), bank[:, 0:2 * JW],
                              mix[0][:, :, :].rearrange("p k n -> p (k n)"))
                elif kind == "values0":
                    lo(v0[1][:, :], bank[:, 0:D], v0[0][:, :])
                    last = lo(v0_tail[TR:2 * TR, :], bank[0:TR, D:2 * D], v0_tail[0:TR, :])
                elif kind == "scores0":
                    t = job[2] % 2
                    dve.tensor_reduce(neg_max0[:, t:t + 1], bank[:, 0:J], AX.X, ALU.max, negate=True)\
                       .then_inc(max0_ready, 1)
                    return
                elif kind == "turn_p0":
                    last = lo(pt0[1][:, :], bank[:, 0:2 * P], pt0[0][:, :])
                elif kind == "attend0":
                    t, par = job[2], job[1] % 2
                    if t == 0:
                        dve.wait_ge(x_rows_in, per.at(lambda c: 16 * (c + 2)))
                    last = dve.tensor_tensor(y_rows[:, par, t, :], bank[:, 0:D], x_rows[:, t, :], ALU.add)
                elif kind == "turn_y":
                    t, par = job[2], job[1] % 2
                    cols = slice(t * P, (t + 1) * P)
                    last = lo(yT[1][:, par, :, cols], bank[:, 0:2 * P].rearrange("p (k n) -> p k n", k=KD),
                              yT[0][:, par, :, cols])
                elif kind == "queries":
                    g, pair = job[2] % 2, job[3]
                    last = lo(qT[1][:, g, pair, :], bank[:, :], qT[0][:, g, pair, :])
                elif kind == "attend":
                    g, pair = job[2] % 2, job[3]
                    last = lo(cT[1][:, g, pair, :], bank[:, :], cT[0][:, g, pair, :])
                elif kind == "values":
                    g = job[2]
                    for q in range(HG):
                        o = (q % 2) * DK
                        r = slice(q * TR, (q + 1) * TR)
                        last = lo(v_tail[1][r, g, o:o + DK], bank[q * TR:(q + 1) * TR, D + q * DK:D + (q + 1) * DK],
                                  v_tail[0][r, g, o:o + DK])
                elif kind == "keys":
                    g = job[2]
                    src = bank[:, 0:2 * JW].rearrange("p (k n) -> p k n", k=2)
                    for a in range(2):
                        r = slice(a * DK, (a + 1) * DK)
                        cols = slice(a * J, (a + 1) * J)
                        last = lo_scaled(keys[1][r, 2 * g:2 * g + 2, cols], src[r, :, 0:J], 1.0 / 8,
                                         keys[0][r, 2 * g:2 * g + 2, cols])
                elif kind == "project":
                    g, half = job[2], job[3]
                    two = slice(2 * half, 2 * half + 2)
                    base = y_rows[:, job[1] % 2, two, :] if g == 0 else acc[:, two, :]
                    last = dve.tensor_tensor(acc[:, two, :], bank[:, :].rearrange("p (t d) -> p t d", t=2),
                                             base, ALU.add)
                last.then_inc(emptied, 1)

            def split_ctx(per):
                dve.wait_ge(ctx_hi, per.at(lambda c: (c + 2) // 2 + 1))
                lo(ctx[1][:, :, :], ctx_raw[:, :, :], ctx[0][:, :, :])
                for k in range(KD):
                    last = lo(ctx_tail[1][:, k, :, :], raw_tail(k), ctx_tail[0][:, k, :, :])
                last.then_inc(ctx_lo, 1)

            def split_x(per):
                dve.wait_ge(x_hi, per.at(lambda c: c + 2))
                lo(xs[1][:, :, :], xT_raw[:, :, :], xs[0][:, :, :]).then_inc(x_lo, 1)

            def tile_stats(per, half):
                dve.wait_ge(emptied, per.done(("project", per.c - 1, G - 1, half)))
                for t in range(2):
                    last = dve.bn_stats(stats[:, half, t, :], acc[:, 2 * half + t, :])
                last.then_inc(stats_ready, 1)

            def moments(per, half):
                for t in range(2):
                    last = dve.bn_aggr(mean_var[:, half, t, :], stats[:, half, t, :])
                last.then_inc(moments_ready, 1)
                dve.wait_ge(moments_ready, per.at(lambda c: 2 * (c - 1) + half + 1))
                dve.tensor_scalar(var_eps[:, half, :], mean_var[:, half, :, 1], EPS, None, ALU.add)\
                   .then_inc(var_ready, 1)

            def centre(per, half):
                dve.wait_ge(rstd_ready, per.at(lambda c: 2 * (c - 1) + half + 1))
                dve.wait_ge(normed_free[half], per.at(lambda c: 16 * (c - 1) + 1))
                for t in range(2):
                    last = dve.tensor_scalar(normed[:, half, t, :], acc[:, 2 * half + t, :],
                                             mean_var[:, half, t, 0:1], rstd[:, half, t:t + 1],
                                             ALU.subtract, ALU.mult)
                last.then_inc(centred, 1)

            def jobs(per, s, place):
                for j in step_jobs(per.c, s)[place]:
                    job(per, j, job_bank[bank_of(j)])

            def period(per):
                for s in range(NS):
                    c, g, t = per.c, s // NT, s % NT
                    if per.summed(s):
                        c1, s1 = per.summed(s)
                        by, t1 = c1 - c, s1 % NT
                        dve.wait_ge(exp_ready, per.at(lambda c: 2 * (NS * (c + by) + s1 + 1)))
                        dve.reciprocal(inv_sums[:, t1, :], sums[:, t1, :]).then_inc(inv_ready, 1)
                    if c == -1 and s == 1:
                        dve.wait_ge(blanked, BLANKED)
                    for n, (w, raw) in enumerate(((wq_s, wq_raw), (wo_s, wo_raw))):
                        if c != -1 or s != WEIGHT_STEPS[n]:
                            continue
                        dve.wait_ge(setup_hi, 4 + n)
                        lo(w[1][:, :, :].rearrange("p k n -> p (k n)"), raw,
                           w[0][:, :, :].rearrange("p k n -> p (k n)")).then_inc(setup_lo, 1)
                    if per.splits_ctx(s):
                        split_ctx(per)
                    if per.splits_x(s):
                        split_x(per)
                    w = per.splits_weights(s)
                    if w is not None:
                        dve.wait_ge(wkv_hi, per.at(lambda c: G * (c + 1) + w + 1))
                        lo(wkv[1][:, :, :], wkv_raw[:, w % 2, :, :], wkv[0][:, :, :]).then_inc(wkv_lo, 1)
                    for half in range(2):
                        if c >= 1 and s == NORM_STEPS[half]:
                            tile_stats(per, half)
                            dve.wait_ge(stats_ready, per.at(lambda c: 2 * (c - 1) + half + 1))
                    jobs(per, s, "first")
                    for half in range(2):
                        if c >= 1 and s == NORM_STEPS[half] + 1:
                            centre(per, half)
                    if per.own and t == NT - 1:
                        dve.wait_ge(tail_hi, per.at(lambda c: G * c + g + 1))
                        lo(pt_tail[1][:, :], turned_tail[:, :], pt_tail[0][:, :]).then_inc(tail_lo, 1)
                    jobs(per, s, "mid")
                    for half in range(2):
                        if c >= 1 and s == NORM_STEPS[half]:
                            moments(per, half)
                    if per.scored(s):
                        c1, s1 = per.scored(s)
                        by, t1 = c1 - c, s1 % NT
                        for pair in range(2):
                            u = 2 * s1 + pair
                            two = score_bank[u % BANKS][:, 0:2 * J].rearrange("p (h j) -> p h j", h=2)
                            dve.wait_ge(scores_ready, per.at(lambda c: 2 * NS * (c + by) + u + 1))
                            if c1 % 2 == 0 and t1 < 2:
                                if c1 == 0 and s1 == 0 and pair == 0:
                                    dve.wait_ge(shaped, 3)
                                dve.tensor_tensor(two, two, mask[:, t1, :].unsqueeze(1).broadcast_to([P, 2, J]),
                                                  ALU.add).then_inc(masked, 1)
                                dve.wait_ge(masked, per.at(
                                    lambda c: 4 * G * ((c + by) // 2) + 4 * (s1 // NT) + 2 * t1 + pair + 1))
                            dve.tensor_reduce(neg_max[:, t1, 2 * pair:2 * pair + 2], two, AX.X, ALU.max,
                                              negate=True).then_inc(max_ready, 1)
                    finish_scores0(per, s)
                    jobs(per, s, "last")

            dve.memset(ctx_raw[:, :, :], 0.0).then_inc(zeroed, 1)
            dve.memset(ident[:, :], 0.0).then_inc(zeroed, 1)
            dve.memset(mask[:, :, :], 0.0).then_inc(zeroed, 1)
            dve.memset(v0_tail[:, :].bitcast(F32), 0.0).then_inc(zeroed, 1)
            dve.memset(probs0[:, :, :], 0.0).then_inc(zeroed, 1)
            dve.memset(minus_half[:, :], -0.5).then_inc(zeroed, 1)
            for n, (dst, src, hi) in enumerate(((wk0_s[1], wk0_raw, wk0_s[0]), (wq0_s[1], wq0_raw, wq0_s[0]),
                                                (wv0_s[1][:, :, :], wv0_raw, wv0_s[0][:, :, :]))):
                dve.wait_ge(setup_hi, n + 1)
                lo(dst, src, hi).then_inc(setup_lo, 1)
                if n == 1:
                    split_ctx(Period(-1))
            split_x(Period(-1))
            for j in SETUP_JOBS:
                job(Period(-1), j, job_bank[bank_of(j)])
            run_periods(dve, period)

        @block.tensor
        def _(pe):
            def product(dst, left, right, start=True, stop=True):
                n = len(left)
                for k in range(n):
                    (lh, ll), (rh, rl) = left[k], right[k]
                    for m, (a, b) in enumerate(((lh, rh), (lh, rl), (ll, rh))):
                        last = pe.matmul(dst, a, b, start=start and k == 0 and m == 0,
                                                stop=stop and k == n - 1 and m == 2,
                                                skip_group_check=not (start and stop))
                return last

            def tiles(pair, cols, *lead):
                return [tuple(part[(slice(None), *lead, k, cols)] for part in pair) for k in range(KD)]

            def tail_tiles():
                return [tuple(part[:, k, :, :].rearrange("p h j -> p (h j)") for part in ctx_tail)
                        for k in range(KD)]

            def job(per, job, bank):
                kind = job[0]
                if JOB[job] >= BANKS:
                    pe.wait_ge(emptied, per.at(lambda c: JOB[per.moved(job, c)] - BANKS + 1))
                if kind == "fold0":
                    pe.wait_ge(setup_lo, 2)
                    for k in range(KD):
                        last = product(bank[:, k * D:(k + 1) * D],
                                       [tuple(w[:, kk, k * P:(k + 1) * P] for w in wk0_s) for kk in range(KD)],
                                       [tuple(w[:, kk, :] for w in wq0_s) for kk in range(KD)])
                elif kind == "values0":
                    if per.c == -1:
                        pe.wait_ge(setup_lo, 3)
                    product(bank[:, 0:D], tiles(ctx, slice(0, P)), tiles(wv0_s, slice(0, D)))
                    last = product(bank[:, D:2 * D], tail_tiles(), tiles(wv0_s, slice(0, D)))
                elif kind == "mix0":
                    if per.c == -1:
                        pe.wait_ge(emptied, JOB[("fold0",)] + 1)
                    pe.wait_ge(ctx_lo, per.at(lambda c: (c + 1) // 2 + 1))
                    for k in range(KD):
                        last = product(bank[:, k * JW:(k + 1) * JW], tiles(fold, slice(k * P, (k + 1) * P)),
                                       tiles(ctx, slice(0, JW)))
                elif kind == "scores0":
                    t = job[2]
                    if t == 0:
                        pe.wait_ge(x_lo, per.at(lambda c: c + 2))
                        if job[1] % 2 == 0:
                            pe.wait_ge(emptied, per.done(("mix0", job[1] // 2)))
                    last = product(bank[:, 0:JW], tiles(xs, slice(t * P, (t + 1) * P)), tiles(mix, slice(0, JW)))
                elif kind == "turn_p0":
                    t = job[2]
                    pe.wait_ge(emptied, per.done(("scores0", job[1], t)))
                    if per.c == -1 and t == 0:
                        pe.wait_ge(shaped, 1)
                    pe.transpose(bank[:, 0:P], probs0[:, t % 2, 0:P], ident[:, :])
                    last = pe.transpose(bank[:, P:2 * P], probs0[:, t % 2, P:2 * P], ident[:, :])
                elif kind == "attend0":
                    pe.wait_ge(emptied, per.done(("turn_p0", job[1], job[2])))
                    dst = bank[:, 0:D]
                    product(dst, [(pt0[0][:, 0:P], pt0[1][:, 0:P])], [(v0[0][:, :], v0[1][:, :])], stop=False)
                    for part in range(2):
                        last = pe.matmul(dst, pt0[part][:, P:2 * P], v0_tail[:, :], start=False,
                                                stop=part == 1, skip_group_check=True)
                elif kind == "turn_y":
                    t, par = job[2], job[1] % 2
                    pe.wait_ge(emptied, per.done(("attend0", job[1], t)))
                    for k in range(KD):
                        last = pe.transpose(bank[:, k * P:(k + 1) * P],
                                                   y_rows[:, par, t, k * P:(k + 1) * P], ident[:, :])
                elif kind == "queries":
                    g, pair, par = job[2], job[3], job[1] % 2
                    if g == 0 and pair == 0:
                        if per.c == -1:
                            pe.wait_ge(setup_lo, 4)
                        pe.wait_ge(emptied, per.done(("turn_y", job[1], NT - 1)))
                    col = (2 * g + pair) * PAIR
                    last = product(bank[:, :], tiles(wq_s, slice(col, col + PAIR)),
                                   tiles(yT, slice(0, CH), par))
                elif kind in ("keys", "values"):
                    b, g = job[1], job[2]
                    pe.wait_ge(wkv_lo, per.at(lambda c: G * (c + 1) + g + 1))
                    if kind == "keys":
                        for pair in range(2):
                            last = product(bank[:, pair * JW:(pair + 1) * JW],
                                           tiles(wkv, slice(pair * PAIR, (pair + 1) * PAIR)),
                                           tiles(ctx, slice(0, JW)))
                    else:
                        product(bank[:, 0:D], tiles(ctx, slice(0, P)), tiles(wkv, slice(0, D)))
                        last = product(bank[:, D:2 * D], tail_tiles(), tiles(wkv, slice(0, D)))
                elif kind == "attend":
                    c, g, pair = job[1], job[2], job[3]
                    by = c - per.c
                    if pair == 0:
                        pe.wait_ge(main_out, per.at(lambda c: NS * (c + by) + NT * (g + 1)))
                        pe.wait_ge(tail_lo, per.at(lambda c: G * (c + by) + g + 1))
                        if c % 2 == 0:
                            pe.wait_ge(emptied, per.done(("values", c // 2, g)))
                    r = slice(pair * DK, (pair + 1) * DK)
                    product(bank[:, :], [(v_tail[0][r, g, :], v_tail[1][r, g, :])],
                            [(pt_tail[0][r, :], pt_tail[1][r, :])], stop=False)
                    for a in range(2):
                        h = 2 * pair + a
                        last = pe.matmul(bank[a * DK:(a + 1) * DK, :],
                                                v_main[:, (HG * g + h) * DK:(HG * g + h + 1) * DK],
                                                pt_main[:, g % 2, h, :], start=False, stop=True,
                                                skip_group_check=True)
                elif kind == "project":
                    c, g, half = job[1], job[2], job[3]
                    by = c - per.c
                    pe.wait_ge(emptied, per.done(("attend", c, g, 1)))
                    if c == 0 and g == 0 and half == 0:
                        pe.wait_ge(setup_lo, 5)
                    for t in range(2):
                        col = (2 * half + t) * P
                        last = product(bank[:, t * D:(t + 1) * D],
                                       [tuple(x[:, g % 2, pair, col:col + P] for x in cT) for pair in range(2)],
                                       [tuple(w[:, 2 * g + pair, :] for w in wo_s) for pair in range(2)])
                last.then_inc(filled, 1)

            def jobs(per, s, place):
                for j in step_jobs(per.c, s)[place]:
                    job(per, j, job_bank[bank_of(j)])

            def turn(per, s):
                g, t = s // NT, s % NT
                pe.wait_ge(probs_ready, per.at(lambda c: NS * c + s + 1))
                if per.c > 0 or s > 0:
                    pe.wait_ge(main_out, per.at(lambda c: NS * c + s))
                for h in range(HG):
                    pe.transpose(turned_main[:, h * P:(h + 1) * P], probs[:, s % 2, h * P:(h + 1) * P],
                                 ident[:, :])
                if t == 0 and (per.c > 0 or g > 0):
                    pe.wait_ge(tail_lo, per.at(lambda c: G * c + g))
                pe.transpose(turned_tail[:, t * P:(t + 1) * P], probs[:, s % 2, HG * P:], ident[:, :])\
                  .then_inc(turned, 1)

            def scores(per, s):
                c1, s1 = per.scored(s)
                by, g, t = c1 - per.c, s1 // NT, s1 % NT
                if t == 0:
                    pe.wait_ge(emptied, per.done(("queries", c1, g, 1)))
                    if c1 % 2 == 0:
                        pe.wait_ge(emptied, per.done(("keys", c1 // 2, g)))
                for pair in range(2):
                    u = 2 * s1 + pair
                    reuse = 2 if u < 2 else BANKS
                    if c1 > 0 or u >= BANKS:
                        pe.wait_ge(exp_ready, per.at(lambda c: 2 * NS * (c + by) + u - reuse + 1))
                    product(score_bank[u % BANKS][:, 0:2 * J],
                            [tuple(q[:, g % 2, pair, t * P:(t + 1) * P] for q in qT)],
                            [tuple(k[:, 2 * g + pair, :] for k in keys)]).then_inc(scores_ready, 1)

            def period(per):
                for s in range(NS):
                    jobs(per, s, "first")
                    if per.own:
                        turn(per, s)
                    jobs(per, s, "mid")
                    if per.scored(s):
                        scores(per, s)
                    jobs(per, s, "last")

            pe.wait_ge(zeroed, ZEROED)
            for j in SETUP_JOBS:
                job(Period(-1), j, job_bank[bank_of(j)])
            run_periods(pe, period)


_NAMES = ("xT", "x", "ctxT", "wq0T", "wk0T", "wv0", "wq", "wk", "wv", "wo", "gamma", "beta")


def kernel(**inputs):
    import numpy as np
    import concourse.bacc as bacc
    from concourse.bass_utils import run_bass_kernel_spmd

    x = np.asarray(inputs["x"]).reshape(B * S, D)
    layouts = {
        "xT": x.T, "x": x, "ctxT": np.asarray(inputs["ctx_1024"]).transpose(0, 2, 1),
        "wq0T": np.asarray(inputs["L0_xattn_Wq"]).T, "wk0T": np.asarray(inputs["L0_xattn_Wk"]).T,
        "wv0": inputs["L0_xattn_Wv"], "wq": inputs["L1_xattn_W_Q"], "wk": inputs["L1_xattn_W_K"],
        "wv": inputs["L1_xattn_W_V"], "wo": inputs["L1_xattn_W_O"],
        "gamma": inputs["L1_xattn_ln_gamma"], "beta": inputs["L1_xattn_ln_beta"],
    }
    nc = bacc.Bacc("TRN2", target_bir_lowering=False, num_devices=1)
    arrays, args = {}, []
    for name in _NAMES:
        a = np.ascontiguousarray(layouts[name])
        arrays[name + "_dram"] = a
        args.append(nc.dram_tensor(name + "_dram", a.shape, mybir.dt.from_np(a.dtype), kind="ExternalInput").ap())
    args.append(nc.dram_tensor("out_dram", (B * S, D), F32, kind="ExternalOutput").ap())
    cross_attention(nc, *args)
    r = run_bass_kernel_spmd(nc, [arrays], core_ids=[0])
    return r.results[0]["out_dram"].reshape(B, S, D)
```

```python
import concourse.bass as bass
from concourse import mybir
from contextlib import ExitStack

F32 = mybir.dt.float32
F32R = mybir.dt.float32r
ALU = mybir.AluOpType
ACT = mybir.ActivationFunctionType
AX = mybir.AxisListType

P = 128
B, S, J, D = 4, 1024, 154, 256
H, DK = 16, 64
KD = D // P
JT = J - P
TR = 32
JP = P + TR
JW = 192
CH = 512
NT = CH // P
NC = B * S // CH
G = 4
HG = H // G
NS = G * NT
PAIR = 2 * DK
EPS = 1e-5
SMALL = 3
MASKED = -1.0e9
ZEROED, BLANKED = 6, 5
JOB_BANKS, SCORE_BANKS = 4, 2


PLACES = ("first", "mid", "last")
SCHEDULE = {
    "project": ((8, "last"), (9, "last"), (12, "last"), (15, "last"),
                (16, "last"), (17, "last"), (20, "last"), (21, "last")),
    "queries": ((-4, "first"), (-4, "first"), (-1, "last"), (-1, "last"),
                (3, "last"), (4, "first"), (7, "last"), (8, "first")),
    "mix0": ((-16, "mid"),),
    "values0": ((-15, "last"),),
    "attend": ((5, "first"), (7, "first"), (9, "first"), (11, "first"),
               (14, "first"), (15, "first"), (17, "first"), (19, "first")),
    "attend0": ((-13, "mid"), (-10, "mid"), (-9, "first"), (-7, "last")),
    "turn_p0": ((-15, "last"), (-12, "mid"), (-10, "mid"), (-8, "last")),
    "turn_y": ((-12, "first"), (-8, "last"), (-9, "last"), (-6, "last")),
    "values": ((3, "last"), (8, "first"), (12, "first"), (14, "first")),
    "scores0": ((-15, "mid"), (-13, "mid"), (-11, "mid"), (-10, "mid")),
    "keys": ((-14, "last"), (-9, "last"), (-4, "first"), (-1, "last")),
}
START = {
    "mix0": ((-16, "last"),),
    "values0": ((-16, "first"),),
    "turn_y": ((-12, "last"), (-11, "last"), (-10, "mid"), (-10, "last")),
    "attend0": ((-13, "mid"), (-12, "mid"), (-11, "mid"), (-10, "mid")),
    "turn_p0": ((-14, "mid"), (-13, "mid"), (-12, "mid"), (-11, "last")),
    "scores0": ((-15, "mid"), (-14, "mid"), (-13, "mid"), (-12, "mid")),
    "queries": ((-7, "first"), (-6, "first"), (-3, "last")),
    "keys": ((-14, "last"), (-10, "last"), (-6, "last"), (-2, "last")),
}
BY_BATCH = ("mix0", "values0", "keys", "values")
BY_TWO = ("attend", "queries", "project")
CTX_STEP, X_STEP = 15, 0
X_ROWS_STEP = 11
WEIGHT_STEPS = (1, 2, 3, 4, 8, 9, 10, 11)
NORM_STEPS = (5, 7)


def step_jobs(c, s):
    at = {place: [] for place in PLACES}
    for kind, entries in SCHEDULE.items():
        for n, (when, place) in enumerate(entries):
            if c == -1:
                when, place = START[kind][n] if n < len(START.get(kind, ())) else (when, place)
            chunk, r = divmod(NS * c + s - when, NS)
            if r or not 0 <= chunk < NC or kind in BY_BATCH and chunk % 2:
                continue
            if kind in BY_BATCH:
                index = (chunk // 2,) + ((n,) if len(entries) > 1 else ())
            else:
                index = (chunk,) + (divmod(n, 2) if kind in BY_TWO else (n,))
            at[place].append((kind,) + index)
    return at


def kv_job_in(c, s):
    for jobs in step_jobs(c, s).values():
        for job in jobs:
            if job[0] in ("keys", "values"):
                return job[2]
    return None


SETUP_JOBS = [("fold0",)]
BY_DVE_ALONE = ("attend0", "project")


def number_jobs():
    order, bank = list(SETUP_JOBS), {job: n for n, job in enumerate(SETUP_JOBS)}
    for c in range(-1, NC + 1):
        for s in range(NS):
            for jobs in step_jobs(c, s).values():
                for job in jobs:
                    bank[job] = (len(order) + c + 1) % JOB_BANKS
                    order.append(job)
    return order, bank


JOBS, BANK = number_jobs()
JOB = {job: k for k, job in enumerate(JOBS)}
ACT_JOB = {job: k for k, job in enumerate(j for j in JOBS if j[0] not in BY_DVE_ALONE)}


def job_before(job):
    for earlier in reversed(JOBS[:JOB[job]]):
        if BANK[earlier] == BANK[job]:
            return earlier
    return None


class Period:

    def __init__(self, c0, i=None):
        self.c, self.i = c0, i

    def at(self, count):
        base = count(self.c)
        if self.i is None:
            return base
        rise = count(self.c + 2) - base
        assert count(self.c + 4) == base + 2 * rise
        return base + self.i * rise if rise else base

    def moved(self, job, c):
        by = c - self.c
        if not by:
            return job
        if job[0] in BY_BATCH:
            by //= 2
        return (job[0], job[1] + by) + job[2:]

    def done(self, job):
        return self.at(lambda c: JOB[self.moved(job, c)] + 1)

    def done_act(self, job):
        return self.at(lambda c: ACT_JOB[self.moved(job, c)] + 1)

    @property
    def own(self):
        return 0 <= self.c < NC

    @property
    def next(self):
        return -1 <= self.c < NC - 1

    def scored(self, s):
        if s + 2 < NS:
            return (self.c, s + 2) if self.own else None
        return (self.c + 1, s + 2 - NS) if self.next else None

    def summed(self, s):
        if s + 1 < NS:
            return (self.c, s + 1) if self.own else None
        return (self.c + 1, s + 1 - NS) if self.next else None

    def splits_weights(self, s):
        return kv_job_in(self.c, s + 1) if s + 1 < NS else None

    def splits_ctx(self, s):
        return s == CTX_STEP and self.c % 2 == 0 and self.own

    def splits_x(self, s):
        return s == X_STEP and self.next and self.c >= 0


def kv_job_before(c, w):
    b = c // 2
    if c % 2 == 1:
        return ("keys", b + 1, w - 1) if w else ("values", b, G - 1)
    return ("values", b, w - 1) if w else ("keys", b, G - 1)


def ends(per, half):
    return per.c == NC and half == 1


def run_periods(engine, period):
    period(Period(-1))
    period(Period(0))
    with engine.Fori(0, (NC - 2) // 2) as i:
        period(Period(1, i))
        period(Period(2, i))
    period(Period(NC - 1))
    period(Period(NC))


def cross_attention(nc, xT, x, ctxT, wq0T, wk0T, wv0, wq, wk, wv, wo, gamma, beta, out):
    es = ExitStack()
    with es:
        def sb(name, shape, dt=F32):
            return es.enter_context(nc.sbuf_tensor(name, shape, dt))

        def sem(name):
            return es.enter_context(nc.semaphore(name))

        def split(name, shape):
            return sb(name + "_hi", shape, F32R), sb(name + "_lo", shape, F32R)

        xT_raw = sb("xT_raw", [P, KD, CH])
        x_rows = sb("x_rows", [P, NT, D])
        ctx_raw = sb("ctx_raw", [P, KD, JW])
        wkv_raw = sb("wkv_raw", [P, KD, D])
        gamma_b = sb("gamma_b", [P, D])
        beta_b = sb("beta_b", [P, D])
        xs = split("xs", [P, KD, CH])
        ctx = split("ctx", [P, KD, JW])
        ctx_tail = split("ctx_tail", [P, KD, HG, TR])
        wkv = split("wkv", [P, KD, D])
        wq_s = split("wq", [P, KD, H * DK])
        wo_s = split("wo", [P, H * DK // P, D])
        wv0_s = split("wv0", [P, KD, D])
        fold = split("fold", [P, KD, D])
        mix = split("mix", [P, KD, JW])
        v0 = split("v0", [P, D])
        v0_tail = sb("v0_tail", [P, D], F32R)
        pt0 = split("pt0", [P, 2 * P])
        yT = split("yT", [P, 2, KD, CH])
        keys = split("keys", [P, H // 2, 2 * J])
        v_main = sb("v_main", [P, H * DK])
        v_tail = split("v_tail", [P, G, PAIR])
        qT = split("qT", [P, 2, 2, CH])
        pt_main = sb("pt_main", [P, 2, HG, CH])
        pt_tail = split("pt_tail", [P, CH])
        cT = split("cT", [P, 2, 2, CH])
        y_rows = sb("y_rows", [P, 2, NT, D])
        acc = sb("acc", [P, NT, D])
        normed = sb("normed", [P, 2, 2, D])
        exps0 = sb("exps0", [P, 2, J])
        probs0 = sb("probs0", [P, 2, 2 * P])
        exps = sb("exps", [P, 2, HG, J])
        probs = sb("probs", [P, 2, HG * JP])
        ident = sb("ident", [P, P])
        mask = sb("mask", [P, 2, J])
        neg_max = sb("neg_max", [P, NT, HG])
        sums = sb("sums", [P, NT, HG])
        inv_sums = sb("inv_sums", [P, NT, HG])
        neg_max0 = sb("neg_max0", [P, 2])
        sums0 = sb("sums0", [P, 2])
        inv_sums0 = sb("inv_sums0", [P, 2])
        stats = sb("stats", [P, 2, 2, 6])
        mean_var = sb("mean_var", [P, 2, 2, 2])
        var_eps = sb("var_eps", [P, 2, 2])
        rstd = sb("rstd", [P, 2, 2])
        minus_half = sb("minus_half", [P, 2])

        wq_raw = pt_main[:, 0, :, :].rearrange("p h n -> p (h n)").rearrange("p (k n) -> p k n", k=KD)
        wo_raw = pt_main[:, 1, :, :].rearrange("p h n -> p (h n)").rearrange("p (k n) -> p k n", n=D)
        wk0_raw = y_rows[:, 0, 0:2, :]
        wq0_raw = y_rows[:, 0, 2:4, :]
        wv0_raw = y_rows[:, 1, 0:2, :]
        wk0_s = [q[:, 0, 0, :].rearrange("p (k n) -> p k n", k=KD) for q in qT]
        wq0_s = [q[:, 0, 1, :].rearrange("p (k n) -> p k n", k=KD) for q in qT]

        def weight_part(n):
            if n < G:
                cols = slice(n * D, (n + 1) * D)
                return (wq_raw[:, :, cols], *(part[:, :, cols] for part in wq_s))
            tiles = slice(2 * (n - G), 2 * (n - G) + 2)
            return (wo_raw[:, tiles, :], *(part[:, tiles, :] for part in wo_s))

        def raw_tail(k):
            return ctx_raw[:, k, P:JP].unsqueeze(1).broadcast_to([P, HG, TR])

        score_bank = [es.enter_context(nc.psum_tensor(f"scores{n}", [P, 512], F32)) for n in range(SCORE_BANKS)]
        job_bank = [es.enter_context(nc.psum_tensor(f"job{n}", [P, 512], F32)) for n in range(JOB_BANKS)]
        turned_main = es.enter_context(nc.psum_tensor("turned_main", [P, 512], F32))
        turned_tail = es.enter_context(nc.psum_tensor("turned_tail", [P, 512], F32))

        small_in = [sem("wk0_in"), sem("wq0_in"), sem("wv0_in")]
        ctx_in = sem("ctx_in")
        xT_in = sem("xT_in")
        x_rows_in = sem("x_rows_in")
        wkv_in = sem("wkv_in")
        wq_in = sem("wq_in")
        wo_in = sem("wo_in")
        affine_in = sem("affine_in")
        normed_free = [sem("normed_free0"), sem("normed_free1")]
        blanked = sem("blanked")
        zeroed = sem("zeroed")
        shaped = sem("shaped")
        setup_hi = sem("setup_hi")
        setup_lo = sem("setup_lo")
        ctx_hi = sem("ctx_hi")
        ctx_lo = sem("ctx_lo")
        x_hi = sem("x_hi")
        x_lo = sem("x_lo")
        wkv_hi = sem("wkv_hi")
        wkv_lo = sem("wkv_lo")
        filled = sem("filled")
        act_part = sem("act_part")
        emptied = sem("emptied")
        max0_ready = sem("max0_ready")
        inv0_ready = sem("inv0_ready")
        scores_ready = sem("scores_ready")
        masked = sem("masked")
        max_ready = sem("max_ready")
        exp_ready = sem("exp_ready")
        inv_ready = sem("inv_ready")
        probs_ready = sem("probs_ready")
        turned = sem("turned")
        main_turned = sem("main_turned")
        main_out = sem("main_out")
        tail_hi = sem("tail_hi")
        tail_lo = sem("tail_lo")
        stats_ready = sem("stats_ready")
        moments_ready = sem("moments_ready")
        var_ready = sem("var_ready")
        rstd_ready = sem("rstd_ready")
        centred = sem("centred")
        scaled = sem("scaled")
        shifted = sem("shifted")
        end_scaled = sem("end_scaled")
        end_shifted = sem("end_shifted")

        xT_v = xT.rearrange("(k p) (c n) -> c p k n", p=P, n=CH)
        x_v = x.rearrange("(c t p) d -> c p t d", p=P, t=NT)
        ctx_v = ctxT.rearrange("b (k p) j -> b p k j", p=P)
        wk_v = wk.rearrange("(k p) (g n) -> g p k n", p=P, n=D)
        wv_v = wv.rearrange("(k p) (g n) -> g p k n", p=P, n=D)
        out_v = out.rearrange("(u t p) d -> u p t d", p=P, t=2)

        block = es.enter_context(nc.Block())

        @block.sync
        def _(sp):
            def ahead(value):
                return value if isinstance(value, int) else sp.snap(value)

            def period(per):
                c, second = per.c, per.c % 2 == 1
                w, next_w = (wk_v, wv_v) if second else (wv_v, wk_v)
                place = {}
                if per.next:
                    place["x"] = ahead(per.at(lambda c: c + 2) % NC)
                if second and per.next:
                    place["ctx"] = ahead(per.at(lambda c: (c + 1) // 2 + 1) % B)
                if c >= 1:
                    place["out"] = [ahead(per.at(lambda c: 2 * (c - 1) + half)) for half in range(2)]
                for s in range(NS):
                    if c == -1 and s == 0:
                        sp.dma_start(wq_raw, wq.rearrange("(k p) n -> p k n", p=P)).then_inc(wq_in, 16)
                        sp.dma_start(wo_raw, wo.rearrange("(k p) n -> p k n", p=P)).then_inc(wo_in, 16)
                    if s == 1 and second and per.next:
                        sp.wait_ge(ctx_lo, per.at(lambda c: (c + 1) // 2 + 1))
                        sp.dma_start(ctx_raw[:, :, 0:J], ctx_v[place["ctx"]]).then_inc(ctx_in, 16)
                    if s == X_STEP + 1 and per.next:
                        sp.wait_ge(x_lo, per.at(lambda c: c + 2))
                        sp.dma_start(xT_raw[:, :, :], xT_v[place["x"]]).then_inc(xT_in, 16)
                    if s == X_ROWS_STEP and per.next:
                        sp.wait_ge(emptied, per.done(("attend0", c + 1, NT - 1)))
                        sp.dma_start(x_rows[:, :, :], x_v[place["x"]]).then_inc(x_rows_in, 16)
                    g = per.splits_weights(s)
                    if g is not None:
                        sp.wait_ge(wkv_lo, per.at(lambda c: G * (c + 1) + g + 1))
                        sp.dma_start(wkv_raw[:, :, :], w[g + 1] if g + 1 < G else next_w[0])\
                          .then_inc(wkv_in, 16)
                    for half in range(2):
                        if c >= 1 and s == NORM_STEPS[half] + 2:
                            if ends(per, half):
                                sp.wait_ge(end_shifted, 1)
                            else:
                                sp.wait_ge(shifted, per.at(lambda c: 2 * (c - 1) + half + 1))
                            sp.dma_start(out_v[place["out"][half]],
                                         normed[:, half, :, :]).then_inc(normed_free[half], 16)
                if c == -1:
                    sp.dma_start(gamma_b[:, :], gamma.partition_broadcast(P)).then_inc(affine_in, 16)
                    sp.dma_start(beta_b[:, :], beta.partition_broadcast(P)).then_inc(affine_in, 16)

            for n, (dst, src) in enumerate(((wk0_raw, wk0T), (wq0_raw, wq0T), (wv0_raw, wv0))):
                sp.dma_start(dst, src.rearrange("(k p) n -> p k n", p=P)).then_inc(small_in[n], 16)
                if n == 1:
                    sp.wait_ge(zeroed, 1)
                    sp.dma_start(ctx_raw[:, :, 0:J], ctx_v[0]).then_inc(ctx_in, 16)
            sp.dma_start(xT_raw[:, :, :], xT_v[0]).then_inc(xT_in, 16)
            sp.dma_start(wkv_raw[:, :, :], wk_v[0]).then_inc(wkv_in, 16)
            sp.dma_start(x_rows[:, :, :], x_v[0]).then_inc(x_rows_in, 16)
            run_periods(sp, period)
            for half in range(2):
                sp.wait_ge(normed_free[half], 16 * NC + 1)
            sp.wait_ge(xT_in, 16 * (NC + 1))
            sp.wait_ge(x_rows_in, 16 * (NC + 1))
            sp.wait_ge(ctx_in, 16 * (B + 1))
            sp.wait_ge(wkv_in, 16 * (G * NC + 1))

        @block.gpsimd
        def _(pool):
            for half in range(2):
                pool.memset(normed[:, half, :, :], 0.0).then_inc(normed_free[half], 1)
            pool.memset(probs[:, :, :], 0.0).then_inc(blanked, 1)
            for blank in (*v_tail, *keys):
                pool.memset(blank[:, :, :].bitcast(F32), 0.0).then_inc(blanked, 1)
            pool.wait_ge(zeroed, 3)
            pool.affine_select(out=ident[:, :], in_=ident[:, :], compare_op=ALU.not_equal, fill=1.0,
                               base=0, pattern=[[-1, P]], channel_multiplier=1).then_inc(shaped, 1)
            for t in range(2):
                pool.affine_select(out=mask[:, t, :], in_=mask[:, t, :], compare_op=ALU.is_ge,
                                   fill=MASKED, base=t * P, pattern=[[-1, J]],
                                   channel_multiplier=1).then_inc(shaped, 1)

            def affine(per, half):
                k = per.at(lambda c: 2 * (c - 1) + half + 1)
                pool.wait_ge(centred, k)
                pool.tensor_tensor(normed[:, half, :, :], normed[:, half, :, :],
                                   gamma_b[:, :].unsqueeze(1).broadcast_to([P, 2, D]), ALU.mult)\
                    .then_inc(scaled, 1)
                pool.wait_ge(scaled, k)
                pool.tensor_tensor(normed[:, half, :, :], normed[:, half, :, :],
                                   beta_b[:, :].unsqueeze(1).broadcast_to([P, 2, D]), ALU.add)\
                    .then_inc(shifted, 1)

            def period(per):
                for s in range(NS):
                    at = per.summed(s)
                    if at:
                        c1, s1 = at
                        by = c1 - per.c
                        t = s1 % NT
                        pool.wait_ge(inv_ready, per.at(lambda c: NS * (c + by) + s1 + 1))
                        if c1 > 0 or s1 >= 2:
                            pool.wait_ge(turned, per.at(lambda c: NS * (c + by) + s1 - 1))
                        o = HG * P
                        for dst, first, keys_in in ((probs[:, s1 % 2, 0:o], 0, P), (probs[:, s1 % 2, o:], P, JT)):
                            dst = dst.rearrange("p (h j) -> p h j", h=HG)[:, :, 0:keys_in]
                            last = pool.tensor_tensor(
                                dst, exps[:, s1 % 2, :, first:first + keys_in],
                                inv_sums[:, t, :].unsqueeze(2).broadcast_to([P, HG, keys_in]), ALU.mult)
                        last.then_inc(probs_ready, 1)
                    for half in range(2):
                        if per.c >= 1 and s == NORM_STEPS[half]:
                            pool.wait_ge(var_ready, per.at(lambda c: 2 * (c - 1) + half + 1))
                            pool.tensor_tensor(rstd[:, half, :], var_eps[:, half, :], minus_half[:, :],
                                               ALU.pow).then_inc(rstd_ready, 1)
                        if per.c >= 1 and s == NORM_STEPS[half] + 1 and not ends(per, half):
                            if per.c == 1 and half == 0:
                                pool.wait_ge(affine_in, 32)
                            affine(per, half)

            run_periods(pool, period)

        @block.scalar
        def _(act):
            def copy(dst, src, scale=1.0):
                return act.activation(dst, src, ACT.Copy, scale=scale)

            def job(per, job, bank):
                kind = job[0]
                if kind in BY_DVE_ALONE:
                    return
                if kind != "scores0":
                    act.wait_ge(filled, per.done(job))
                if kind == "fold0":
                    last = copy(fold[0][:, :, :], bank[:, :].rearrange("p (k n) -> p k n", k=KD), 1.0 / 16)
                elif kind == "mix0":
                    last = copy(mix[0][:, :, :], bank[:, 0:2 * JW].rearrange("p (k n) -> p k n", k=KD))
                elif kind == "values0":
                    copy(v0[0][:, :], bank[:, 0:D])
                    last = copy(v0_tail[0:TR, :], bank[0:TR, D:2 * D])
                elif kind == "scores0":
                    t = job[2]
                    act.wait_ge(max0_ready, per.at(lambda c: NT * (c + 1) + t + 1))
                    last = act.activation(exps0[:, t % 2, :], bank[:, 0:J], ACT.Exp,
                                          bias=neg_max0[:, t % 2:t % 2 + 1],
                                          accum_out=sums0[:, t % 2:t % 2 + 1])
                elif kind == "turn_p0":
                    last = copy(pt0[0][:, :], bank[:, 0:2 * P])
                elif kind == "turn_y":
                    t, par = job[2], job[1] % 2
                    last = copy(yT[0][:, par, :, t * P:(t + 1) * P],
                                bank[:, 0:2 * P].rearrange("p (k n) -> p k n", k=KD))
                elif kind == "queries":
                    last = copy(qT[0][:, job[2] % 2, job[3], :], bank[:, :])
                elif kind == "attend":
                    last = copy(cT[0][:, job[2] % 2, job[3], :], bank[:, :])
                elif kind == "values":
                    g = job[2]
                    copy(v_main[:, g * D:(g + 1) * D], bank[:, 0:D])
                    for q in range(HG):
                        o = (q % 2) * DK
                        last = copy(v_tail[0][q * TR:(q + 1) * TR, g, o:o + DK],
                                    bank[q * TR:(q + 1) * TR, D + q * DK:D + (q + 1) * DK])
                elif kind == "keys":
                    g = job[2]
                    src = bank[:, 0:2 * JW].rearrange("p (k n) -> p k n", k=2)
                    for a in range(2):
                        r = slice(a * DK, (a + 1) * DK)
                        last = copy(keys[0][r, 2 * g:2 * g + 2, a * J:(a + 1) * J], src[r, :, 0:J], 1.0 / 8)
                last.then_inc(act_part, 1)

            def split_ctx(per):
                act.wait_ge(ctx_in, per.at(lambda c: 16 * ((c + 2) // 2 + 1)))
                copy(ctx[0][:, :, :], ctx_raw[:, :, :])
                for k in range(KD):
                    last = copy(ctx_tail[0][:, k, :, :], raw_tail(k))
                last.then_inc(ctx_hi, 1)

            def split_x(per):
                act.wait_ge(xT_in, per.at(lambda c: 16 * (c + 2)))
                copy(xs[0][:, :, :], xT_raw[:, :, :]).then_inc(x_hi, 1)

            def jobs(per, s, place):
                for j in step_jobs(per.c, s)[place]:
                    job(per, j, job_bank[BANK[j]])

            def period(per):
                for s in range(NS):
                    c, g, t = per.c, s // NT, s % NT
                    if c == -1 and s == 1:
                        act.wait_ge(blanked, BLANKED)
                    for n, when in enumerate(WEIGHT_STEPS):
                        if c == -1 and s == when:
                            act.wait_ge((wq_in, wo_in)[n // G], 16)
                            raw, hi, _ = weight_part(n)
                            copy(hi, raw).then_inc(setup_hi, 1)
                    if per.splits_ctx(s):
                        split_ctx(per)
                    if per.splits_x(s):
                        split_x(per)
                    w = per.splits_weights(s)
                    if w is not None:
                        if kv_job_before(c, w) in JOB:
                            act.wait_ge(filled, per.done(kv_job_before(c, w)))
                        act.wait_ge(wkv_in, per.at(lambda c: 16 * (G * (c + 1) + w + 1)))
                        copy(wkv[0][:, :, :], wkv_raw[:, :, :]).then_inc(wkv_hi, 1)
                    jobs(per, s, "first")
                    if per.own:
                        act.wait_ge(main_turned, per.at(lambda c: NS * c + s + 1))
                        if c == 0 and s == 0:
                            act.wait_ge(setup_lo, SMALL + 2 * G)
                        if t == 0:
                            over = ("attend", c, g - 2, 1) if g >= 2 else ("attend", c - 1, g + 2, 1)
                            if over in JOB:
                                act.wait_ge(filled, per.done(over))
                        copy(pt_main[:, g % 2, :, t * P:(t + 1) * P],
                             turned_main[:, :].rearrange("p (h n) -> p h n", h=HG)).then_inc(main_out, 1)
                        if t == NT - 1:
                            act.wait_ge(turned, per.at(lambda c: NS * c + s + 1))
                            over = ("attend", c, g - 1, 1) if g >= 1 else ("attend", c - 1, G - 1, 1)
                            if over in JOB:
                                act.wait_ge(filled, per.done(over))
                            copy(pt_tail[0][:, :], turned_tail[:, :]).then_inc(tail_hi, 1)
                    jobs(per, s, "mid")
                    if per.scored(s):
                        c1, s1 = per.scored(s)
                        by = c1 - c
                        t1 = s1 % NT
                        for pair in range(2):
                            u = 2 * s1 + pair
                            if pair == 0 and (c1 > 0 or s1 >= 2):
                                act.wait_ge(probs_ready, per.at(lambda c: NS * (c + by) + s1 - 1))
                            act.wait_ge(max_ready, per.at(lambda c: 2 * NS * (c + by) + u + 1))
                            for a in range(2):
                                h = 2 * pair + a
                                last = act.activation(
                                    exps[:, s1 % 2, h, :], score_bank[u % SCORE_BANKS][:, a * J:(a + 1) * J],
                                    ACT.Exp, bias=neg_max[:, t1, h:h + 1], accum_out=sums[:, t1, h:h + 1])
                            last.then_inc(exp_ready, 1)
                    jobs(per, s, "last")

            for n, (dst, src) in enumerate(((wk0_s[0], wk0_raw), (wq0_s[0], wq0_raw), (wv0_s[0][:, :, :], wv0_raw))):
                act.wait_ge(small_in[n], 16)
                copy(dst, src).then_inc(setup_hi, 1)
                if n == 1:
                    split_ctx(Period(-1))
            split_x(Period(-1))
            for j in SETUP_JOBS:
                job(Period(-1), j, job_bank[BANK[j]])
            run_periods(act, period)

        @block.vector
        def _(dve):
            def lo(dst, whole, hi):
                return dve.tensor_tensor(dst, whole, hi.bitcast(F32), ALU.subtract)

            def lo_scaled(dst, whole, scale, hi):
                return dve.scalar_tensor_tensor(dst, whole, scale, hi.bitcast(F32), ALU.mult, ALU.subtract)

            def finish_scores0(per, s):
                at = step_jobs(per.c, s)
                for j in at["first"] + at["mid"]:
                    if j[0] == "scores0":
                        t = j[2] % 2
                        dve.wait_ge(act_part, per.done_act(j))
                        dve.reciprocal(inv_sums0[:, t:t + 1], sums0[:, t:t + 1]).then_inc(inv0_ready, 1)
                        dve.wait_ge(inv0_ready, per.at(lambda c: NT * (c + 1) + j[2] + 1))
                        dve.tensor_scalar(probs0[:, t, 0:P], exps0[:, t, 0:P], inv_sums0[:, t:t + 1],
                                          None, ALU.mult)
                        dve.tensor_scalar(
                            probs0[:, t, P:].rearrange("p (r j) -> p r j", j=TR)[:, :, 0:JT],
                            exps0[:, t, P:J].unsqueeze(1).broadcast_to([P, P // TR, JT]),
                            inv_sums0[:, t:t + 1], None, ALU.mult).then_inc(emptied, 1)

            def job(per, job, bank):
                kind = job[0]
                if kind in BY_DVE_ALONE or kind == "scores0":
                    dve.wait_ge(filled, per.done(job))
                else:
                    dve.wait_ge(act_part, per.done_act(job))
                if kind == "fold0":
                    last = lo_scaled(fold[1][:, :, :].rearrange("p k n -> p (k n)"), bank[:, :], 1.0 / 16,
                                     fold[0][:, :, :].rearrange("p k n -> p (k n)"))
                elif kind == "mix0":
                    last = lo(mix[1][:, :, :].rearrange("p k n -> p (k n)"), bank[:, 0:2 * JW],
                              mix[0][:, :, :].rearrange("p k n -> p (k n)"))
                elif kind == "values0":
                    lo(v0[1][:, :], bank[:, 0:D], v0[0][:, :])
                    last = lo(v0_tail[TR:2 * TR, :], bank[0:TR, D:2 * D], v0_tail[0:TR, :])
                elif kind == "scores0":
                    t = job[2] % 2
                    dve.tensor_reduce(neg_max0[:, t:t + 1], bank[:, 0:J], AX.X, ALU.max, negate=True)\
                       .then_inc(max0_ready, 1)
                    return
                elif kind == "turn_p0":
                    last = lo(pt0[1][:, :], bank[:, 0:2 * P], pt0[0][:, :])
                elif kind == "attend0":
                    t, par = job[2], job[1] % 2
                    if t == 0:
                        dve.wait_ge(x_rows_in, per.at(lambda c: 16 * (c + 2)))
                    last = dve.tensor_tensor(y_rows[:, par, t, :], bank[:, 0:D], x_rows[:, t, :], ALU.add)
                elif kind == "turn_y":
                    t, par = job[2], job[1] % 2
                    cols = slice(t * P, (t + 1) * P)
                    last = lo(yT[1][:, par, :, cols], bank[:, 0:2 * P].rearrange("p (k n) -> p k n", k=KD),
                              yT[0][:, par, :, cols])
                elif kind == "queries":
                    g, pair = job[2] % 2, job[3]
                    last = lo(qT[1][:, g, pair, :], bank[:, :], qT[0][:, g, pair, :])
                elif kind == "attend":
                    g, pair = job[2] % 2, job[3]
                    last = lo(cT[1][:, g, pair, :], bank[:, :], cT[0][:, g, pair, :])
                elif kind == "values":
                    g = job[2]
                    for q in range(HG):
                        o = (q % 2) * DK
                        r = slice(q * TR, (q + 1) * TR)
                        last = lo(v_tail[1][r, g, o:o + DK], bank[q * TR:(q + 1) * TR, D + q * DK:D + (q + 1) * DK],
                                  v_tail[0][r, g, o:o + DK])
                elif kind == "keys":
                    g = job[2]
                    src = bank[:, 0:2 * JW].rearrange("p (k n) -> p k n", k=2)
                    for a in range(2):
                        r = slice(a * DK, (a + 1) * DK)
                        cols = slice(a * J, (a + 1) * J)
                        last = lo_scaled(keys[1][r, 2 * g:2 * g + 2, cols], src[r, :, 0:J], 1.0 / 8,
                                         keys[0][r, 2 * g:2 * g + 2, cols])
                elif kind == "project":
                    g, half = job[2], job[3]
                    two = slice(2 * half, 2 * half + 2)
                    base = y_rows[:, job[1] % 2, two, :] if g == 0 else acc[:, two, :]
                    last = dve.tensor_tensor(acc[:, two, :], bank[:, :].rearrange("p (t d) -> p t d", t=2),
                                             base, ALU.add)
                last.then_inc(emptied, 1)

            def split_ctx(per):
                dve.wait_ge(ctx_hi, per.at(lambda c: (c + 2) // 2 + 1))
                lo(ctx[1][:, :, :], ctx_raw[:, :, :], ctx[0][:, :, :])
                for k in range(KD):
                    last = lo(ctx_tail[1][:, k, :, :], raw_tail(k), ctx_tail[0][:, k, :, :])
                last.then_inc(ctx_lo, 1)

            def split_x(per):
                dve.wait_ge(x_hi, per.at(lambda c: c + 2))
                lo(xs[1][:, :, :], xT_raw[:, :, :], xs[0][:, :, :]).then_inc(x_lo, 1)

            def tile_stats(per, half):
                dve.wait_ge(emptied, per.done(("project", per.c - 1, G - 1, half)))
                for t in range(2):
                    last = dve.bn_stats(stats[:, half, t, :], acc[:, 2 * half + t, :])
                last.then_inc(stats_ready, 1)

            def moments(per, half):
                for t in range(2):
                    last = dve.bn_aggr(mean_var[:, half, t, :], stats[:, half, t, :])
                last.then_inc(moments_ready, 1)
                dve.wait_ge(moments_ready, per.at(lambda c: 2 * (c - 1) + half + 1))
                dve.tensor_scalar(var_eps[:, half, :], mean_var[:, half, :, 1], EPS, None, ALU.add)\
                   .then_inc(var_ready, 1)

            def affine_at_end(half):
                both = normed[:, half, :, :]
                dve.wait_ge(affine_in, 32)
                dve.wait_ge(centred, 2 * NC)
                dve.tensor_tensor(both, both, gamma_b[:, :].unsqueeze(1).broadcast_to([P, 2, D]), ALU.mult)\
                   .then_inc(end_scaled, 1)
                dve.wait_ge(end_scaled, 1)
                dve.tensor_tensor(both, both, beta_b[:, :].unsqueeze(1).broadcast_to([P, 2, D]), ALU.add)\
                   .then_inc(end_shifted, 1)

            def centre(per, half):
                dve.wait_ge(rstd_ready, per.at(lambda c: 2 * (c - 1) + half + 1))
                dve.wait_ge(normed_free[half], per.at(lambda c: 16 * (c - 1) + 1))
                for t in range(2):
                    last = dve.tensor_scalar(normed[:, half, t, :], acc[:, 2 * half + t, :],
                                             mean_var[:, half, t, 0:1], rstd[:, half, t:t + 1],
                                             ALU.subtract, ALU.mult)
                last.then_inc(centred, 1)

            def jobs(per, s, place):
                for j in step_jobs(per.c, s)[place]:
                    job(per, j, job_bank[BANK[j]])

            def period(per):
                for s in range(NS):
                    c, g, t = per.c, s // NT, s % NT
                    if per.summed(s):
                        c1, s1 = per.summed(s)
                        by, t1 = c1 - c, s1 % NT
                        dve.wait_ge(exp_ready, per.at(lambda c: 2 * (NS * (c + by) + s1 + 1)))
                        dve.reciprocal(inv_sums[:, t1, :], sums[:, t1, :]).then_inc(inv_ready, 1)
                    if c == -1 and s == 1:
                        dve.wait_ge(blanked, BLANKED)
                    for n, when in enumerate(WEIGHT_STEPS):
                        if c == -1 and s == when:
                            raw, hi, low = weight_part(n)
                            dve.wait_ge(setup_hi, SMALL + n + 1)
                            lo(low, raw, hi).then_inc(setup_lo, 1)
                    if per.splits_ctx(s):
                        split_ctx(per)
                    if per.splits_x(s):
                        split_x(per)
                    w = per.splits_weights(s)
                    if w is not None:
                        dve.wait_ge(wkv_hi, per.at(lambda c: G * (c + 1) + w + 1))
                        lo(wkv[1][:, :, :], wkv_raw[:, :, :], wkv[0][:, :, :]).then_inc(wkv_lo, 1)
                    for half in range(2):
                        if c >= 1 and s == NORM_STEPS[half]:
                            tile_stats(per, half)
                            dve.wait_ge(stats_ready, per.at(lambda c: 2 * (c - 1) + half + 1))
                    jobs(per, s, "first")
                    for half in range(2):
                        if c >= 1 and s == NORM_STEPS[half] + 1:
                            centre(per, half)
                            if ends(per, half):
                                affine_at_end(half)
                    jobs(per, s, "mid")
                    if per.own and t == NT - 1:
                        dve.wait_ge(tail_hi, per.at(lambda c: G * c + g + 1))
                        lo(pt_tail[1][:, :], turned_tail[:, :], pt_tail[0][:, :]).then_inc(tail_lo, 1)
                    for half in range(2):
                        if c >= 1 and s == NORM_STEPS[half]:
                            moments(per, half)
                    if per.scored(s):
                        c1, s1 = per.scored(s)
                        by, t1 = c1 - c, s1 % NT
                        for pair in range(2):
                            u = 2 * s1 + pair
                            two = score_bank[u % SCORE_BANKS][:, 0:2 * J].rearrange("p (h j) -> p h j", h=2)
                            dve.wait_ge(scores_ready, per.at(lambda c: 2 * NS * (c + by) + u + 1))
                            if c1 % 2 == 0 and t1 < 2:
                                if c1 == 0 and s1 == 0 and pair == 0:
                                    dve.wait_ge(shaped, 3)
                                part = two[:, :, t1 * P:J]
                                dve.tensor_tensor(
                                    part, part,
                                    mask[:, t1, t1 * P:J].unsqueeze(1).broadcast_to([P, 2, J - t1 * P]),
                                    ALU.add).then_inc(masked, 1)
                                dve.wait_ge(masked, per.at(
                                    lambda c: 4 * G * ((c + by) // 2) + 4 * (s1 // NT) + 2 * t1 + pair + 1))
                            dve.tensor_reduce(neg_max[:, t1, 2 * pair:2 * pair + 2], two, AX.X, ALU.max,
                                              negate=True).then_inc(max_ready, 1)
                    finish_scores0(per, s)
                    jobs(per, s, "last")

            dve.memset(ctx_raw[:, :, :], 0.0).then_inc(zeroed, 1)
            dve.memset(ident[:, :], 0.0).then_inc(zeroed, 1)
            dve.memset(mask[:, :, :], 0.0).then_inc(zeroed, 1)
            dve.memset(v0_tail[:, :].bitcast(F32), 0.0).then_inc(zeroed, 1)
            dve.memset(probs0[:, :, :], 0.0).then_inc(zeroed, 1)
            dve.memset(minus_half[:, :], -0.5).then_inc(zeroed, 1)
            for n, (dst, src, hi) in enumerate(((wk0_s[1], wk0_raw, wk0_s[0]), (wq0_s[1], wq0_raw, wq0_s[0]),
                                                (wv0_s[1][:, :, :], wv0_raw, wv0_s[0][:, :, :]))):
                dve.wait_ge(setup_hi, n + 1)
                lo(dst, src, hi).then_inc(setup_lo, 1)
                if n == 1:
                    split_ctx(Period(-1))
            split_x(Period(-1))
            for j in SETUP_JOBS:
                job(Period(-1), j, job_bank[BANK[j]])
            run_periods(dve, period)

        @block.tensor
        def _(pe):
            def product(dst, left, right, start=True, stop=True):
                n = len(left)
                for k in range(n):
                    (lh, ll), (rh, rl) = left[k], right[k]
                    for m, (a, b) in enumerate(((lh, rh), (lh, rl), (ll, rh))):
                        last = pe.matmul(dst, a, b, start=start and k == 0 and m == 0,
                                                stop=stop and k == n - 1 and m == 2,
                                                skip_group_check=not (start and stop))
                return last

            def tiles(pair, cols, *lead):
                return [tuple(part[(slice(None), *lead, k, cols)] for part in pair) for k in range(KD)]

            def tail_tiles():
                return [tuple(part[:, k, :, :].rearrange("p h j -> p (h j)") for part in ctx_tail)
                        for k in range(KD)]

            def job(per, job, bank):
                kind = job[0]
                if job_before(job):
                    pe.wait_ge(emptied, per.at(lambda c: JOB[job_before(per.moved(job, c))] + 1))
                if kind == "fold0":
                    pe.wait_ge(setup_lo, 2)
                    for k in range(KD):
                        last = product(bank[:, k * D:(k + 1) * D],
                                       [tuple(w[:, kk, k * P:(k + 1) * P] for w in wk0_s) for kk in range(KD)],
                                       [tuple(w[:, kk, :] for w in wq0_s) for kk in range(KD)])
                elif kind == "values0":
                    if per.c == -1:
                        pe.wait_ge(setup_lo, 3)
                    product(bank[:, 0:D], tiles(ctx, slice(0, P)), tiles(wv0_s, slice(0, D)))
                    last = product(bank[:, D:2 * D], tail_tiles(), tiles(wv0_s, slice(0, D)))
                elif kind == "mix0":
                    if per.c == -1:
                        pe.wait_ge(emptied, JOB[("fold0",)] + 1)
                    pe.wait_ge(ctx_lo, per.at(lambda c: (c + 1) // 2 + 1))
                    for k in range(KD):
                        last = product(bank[:, k * JW:(k + 1) * JW], tiles(fold, slice(k * P, (k + 1) * P)),
                                       tiles(ctx, slice(0, JW)))
                elif kind == "scores0":
                    t = job[2]
                    if t == 0:
                        pe.wait_ge(x_lo, per.at(lambda c: c + 2))
                        if job[1] % 2 == 0:
                            pe.wait_ge(emptied, per.done(("mix0", job[1] // 2)))
                    last = product(bank[:, 0:JW], tiles(xs, slice(t * P, (t + 1) * P)), tiles(mix, slice(0, JW)))
                elif kind == "turn_p0":
                    t = job[2]
                    pe.wait_ge(emptied, per.done(("scores0", job[1], t)))
                    if per.c == -1 and t == 0:
                        pe.wait_ge(shaped, 1)
                    pe.transpose(bank[:, 0:P], probs0[:, t % 2, 0:P], ident[:, :])
                    last = pe.transpose(bank[:, P:2 * P], probs0[:, t % 2, P:2 * P], ident[:, :])
                elif kind == "attend0":
                    pe.wait_ge(emptied, per.done(("turn_p0", job[1], job[2])))
                    dst = bank[:, 0:D]
                    product(dst, [(pt0[0][:, 0:P], pt0[1][:, 0:P])], [(v0[0][:, :], v0[1][:, :])], stop=False)
                    for part in range(2):
                        last = pe.matmul(dst, pt0[part][:, P:2 * P], v0_tail[:, :], start=False,
                                                stop=part == 1, skip_group_check=True)
                elif kind == "turn_y":
                    t, par = job[2], job[1] % 2
                    pe.wait_ge(emptied, per.done(("attend0", job[1], t)))
                    for k in range(KD):
                        last = pe.transpose(bank[:, k * P:(k + 1) * P],
                                                   y_rows[:, par, t, k * P:(k + 1) * P], ident[:, :])
                elif kind == "queries":
                    g, pair, par = job[2], job[3], job[1] % 2
                    if job[1] == 0 and pair == 0:
                        pe.wait_ge(setup_lo, SMALL + g + 1)
                    if g == 0 and pair == 0:
                        pe.wait_ge(emptied, per.done(("turn_y", job[1], NT - 1)))
                    col = (2 * g + pair) * PAIR
                    last = product(bank[:, :], tiles(wq_s, slice(col, col + PAIR)),
                                   tiles(yT, slice(0, CH), par))
                elif kind in ("keys", "values"):
                    b, g = job[1], job[2]
                    pe.wait_ge(wkv_lo, per.at(lambda c: G * (c + 1) + g + 1))
                    if kind == "keys":
                        for pair in range(2):
                            last = product(bank[:, pair * JW:(pair + 1) * JW],
                                           tiles(wkv, slice(pair * PAIR, (pair + 1) * PAIR)),
                                           tiles(ctx, slice(0, JW)))
                    else:
                        product(bank[:, 0:D], tiles(ctx, slice(0, P)), tiles(wkv, slice(0, D)))
                        last = product(bank[:, D:2 * D], tail_tiles(), tiles(wkv, slice(0, D)))
                elif kind == "attend":
                    c, g, pair = job[1], job[2], job[3]
                    by = c - per.c
                    if pair == 0:
                        pe.wait_ge(main_out, per.at(lambda c: NS * (c + by) + NT * (g + 1)))
                        pe.wait_ge(tail_lo, per.at(lambda c: G * (c + by) + g + 1))
                        if c % 2 == 0:
                            pe.wait_ge(emptied, per.done(("values", c // 2, g)))
                    r = slice(pair * DK, (pair + 1) * DK)
                    product(bank[:, :], [(v_tail[0][r, g, :], v_tail[1][r, g, :])],
                            [(pt_tail[0][r, :], pt_tail[1][r, :])], stop=False)
                    for a in range(2):
                        h = 2 * pair + a
                        last = pe.matmul(bank[a * DK:(a + 1) * DK, :],
                                                v_main[:, (HG * g + h) * DK:(HG * g + h + 1) * DK],
                                                pt_main[:, g % 2, h, :], start=False, stop=True,
                                                skip_group_check=True)
                elif kind == "project":
                    c, g, half = job[1], job[2], job[3]
                    by = c - per.c
                    pe.wait_ge(emptied, per.done(("attend", c, g, 1)))
                    if c == 0 and half == 0:
                        pe.wait_ge(setup_lo, SMALL + G + g + 1)
                    for t in range(2):
                        col = (2 * half + t) * P
                        last = product(bank[:, t * D:(t + 1) * D],
                                       [tuple(x[:, g % 2, pair, col:col + P] for x in cT) for pair in range(2)],
                                       [tuple(w[:, 2 * g + pair, :] for w in wo_s) for pair in range(2)])
                last.then_inc(filled, 1)

            def jobs(per, s, place):
                for j in step_jobs(per.c, s)[place]:
                    job(per, j, job_bank[BANK[j]])

            def turn(per, s):
                g, t = s // NT, s % NT
                pe.wait_ge(probs_ready, per.at(lambda c: NS * c + s + 1))
                if per.c > 0 or s > 0:
                    pe.wait_ge(main_out, per.at(lambda c: NS * c + s))
                for h in range(HG):
                    last = pe.transpose(turned_main[:, h * P:(h + 1) * P], probs[:, s % 2, h * P:(h + 1) * P],
                                        ident[:, :])
                last.then_inc(main_turned, 1)
                if t == 0 and (per.c > 0 or g > 0):
                    pe.wait_ge(tail_lo, per.at(lambda c: G * c + g))
                pe.transpose(turned_tail[:, t * P:(t + 1) * P], probs[:, s % 2, HG * P:], ident[:, :])\
                  .then_inc(turned, 1)

            def scores(per, s):
                c1, s1 = per.scored(s)
                by, g, t = c1 - per.c, s1 // NT, s1 % NT
                if t == 0:
                    pe.wait_ge(emptied, per.done(("queries", c1, g, 1)))
                    if c1 % 2 == 0:
                        pe.wait_ge(emptied, per.done(("keys", c1 // 2, g)))
                for pair in range(2):
                    u = 2 * s1 + pair
                    if c1 > 0 or u >= SCORE_BANKS:
                        pe.wait_ge(exp_ready, per.at(lambda c: 2 * NS * (c + by) + u - SCORE_BANKS + 1))
                    product(score_bank[u % SCORE_BANKS][:, 0:2 * J],
                            [tuple(q[:, g % 2, pair, t * P:(t + 1) * P] for q in qT)],
                            [tuple(k[:, 2 * g + pair, :] for k in keys)]).then_inc(scores_ready, 1)

            def period(per):
                for s in range(NS):
                    jobs(per, s, "first")
                    if per.own:
                        turn(per, s)
                    jobs(per, s, "mid")
                    if per.scored(s):
                        scores(per, s)
                    jobs(per, s, "last")

            pe.wait_ge(zeroed, ZEROED)
            for j in SETUP_JOBS:
                job(Period(-1), j, job_bank[BANK[j]])
            run_periods(pe, period)


_NAMES = ("xT", "x", "ctxT", "wq0T", "wk0T", "wv0", "wq", "wk", "wv", "wo", "gamma", "beta")


def kernel(**inputs):
    import numpy as np
    import concourse.bacc as bacc
    from concourse.bass_utils import run_bass_kernel_spmd

    x = np.asarray(inputs["x"]).reshape(B * S, D)
    layouts = {
        "xT": x.T, "x": x, "ctxT": np.asarray(inputs["ctx_1024"]).transpose(0, 2, 1),
        "wq0T": np.asarray(inputs["L0_xattn_Wq"]).T, "wk0T": np.asarray(inputs["L0_xattn_Wk"]).T,
        "wv0": inputs["L0_xattn_Wv"], "wq": inputs["L1_xattn_W_Q"], "wk": inputs["L1_xattn_W_K"],
        "wv": inputs["L1_xattn_W_V"], "wo": inputs["L1_xattn_W_O"],
        "gamma": inputs["L1_xattn_ln_gamma"], "beta": inputs["L1_xattn_ln_beta"],
    }
    nc = bacc.Bacc("TRN2", target_bir_lowering=False, num_devices=1)
    arrays, args = {}, []
    for name in _NAMES:
        a = np.ascontiguousarray(layouts[name])
        arrays[name + "_dram"] = a
        args.append(nc.dram_tensor(name + "_dram", a.shape, mybir.dt.from_np(a.dtype), kind="ExternalInput").ap())
    args.append(nc.dram_tensor("out_dram", (B * S, D), F32, kind="ExternalOutput").ap())
    cross_attention(nc, *args)
    r = run_bass_kernel_spmd(nc, [arrays], core_ids=[0])
    return r.results[0]["out_dram"].reshape(B, S, D)
```
